# Optimizing a Trainium2 kernel written in Bass

```python
import numpy as np
import jax
import jax.numpy as jnp

def _softmax(x, axis=-1):
    return jax.nn.softmax(x, axis=axis)

def _gelu(x):
    return jax.nn.gelu(x, approximate=True)

def _silu(x):
    return jax.nn.silu(x)

def _sigmoid(x):
    return jax.nn.sigmoid(x)

def _layernorm(x, axis=-1, eps=1e-05):
    m = jnp.mean(x, axis=axis, keepdims=True)
    v = jnp.var(x, axis=axis, keepdims=True)
    return (x - m) / jnp.sqrt(v + eps)

def _scatter_add(tgt, idx, src, axis=0):
    return tgt.at[idx].add(src)

def _segment_sum(src, seg, n):
    return jax.ops.segment_sum(src, seg, n)
kernel_name = 'mk_cond_resid_d4_seqx_r4_a94a6c'

def setup_inputs(seed: int=0):
    np.random.seed(seed)
    _w = jnp.asarray

    def _rec_inputs():
        import jax
        import jax.numpy as jnp
        _rk = jax.random.key(seed)
        x = 7.22e-05 + 1 * jax.random.normal(jax.random.fold_in(_rk, 1), (4, 512, 256), jnp.float32)
        _lenS = 512 - jax.random.randint(jax.random.fold_in(_rk, 7), (4,), 0, max(1, 512 // 4) + 1, jnp.int32)
        _lenS2 = 512 - jax.random.randint(jax.random.fold_in(_rk, 8), (4,), 0, max(1, 512 // 4) + 1, jnp.int32)
        cond_8 = -0.104238 + 1.01173 * jax.random.normal(jax.random.fold_in(_rk, 11), (4, 8), jnp.float32)
        return (x, cond_8)
    x, cond_8 = _rec_inputs()

    def _L0_cond_setup():
        import jax, jax.numpy as jnp
        import numpy as np
        TOP_K = 2
        NUM_MOE_LAYERS = 12

        def _gemma_mlp(x, gate_w, up_w, down_w):
            g = jnp.einsum('bsh,hi->bsi', x, gate_w)
            u = jnp.einsum('bsh,hi->bsi', x, up_w)
            return jnp.einsum('bsi,ih->bsh', jax.nn.gelu(g, approximate=True) * u, down_w)
        key = jax.random.key(seed)
        ks = jax.random.split(key, 8)
        B, S, H, I, E = (32, 64, 256, 1024, 8)
        std = 0.02
        return {'x': jax.random.normal(ks[0], (B, S, H), jnp.float32), 'router_logits': jax.random.normal(ks[1], (B, E), jnp.float32), 'skill_gate': jax.random.normal(ks[2], (E, H, I), jnp.float32) * std, 'skill_up': jax.random.normal(ks[3], (E, H, I), jnp.float32) * std, 'skill_down': jax.random.normal(ks[4], (E, I, H), jnp.float32) * std, 'shared_gate': jax.random.normal(ks[5], (H, I), jnp.float32) * std, 'shared_up': jax.random.normal(ks[6], (H, I), jnp.float32) * std, 'shared_down': jax.random.normal(ks[7], (I, H), jnp.float32) * std}
    _L0_cond_all = _L0_cond_setup()
    _L0_cond_in = {k: v for k, v in _L0_cond_all.items() if k in ('skill_gate', 'skill_up', 'skill_down', 'shared_gate', 'shared_up', 'shared_down')}
    del _L0_cond_all

    def _L1_cond_setup():
        import jax, jax.numpy as jnp
        import numpy as np
        B, S, D = (16, 512, 256)
        E, H = (8, 512)
        key = jax.random.key(seed)
        ks = jax.random.split(key, 8)
        scale = 0.02
        x = jax.random.normal(ks[0], (B, S, D), dtype=jnp.float32)
        opcode_onehot = jax.random.uniform(ks[1], (B, E), dtype=jnp.float32)
        W_up = jax.random.normal(ks[2], (E, H, D), dtype=jnp.float32) * scale
        b_up = jnp.zeros((E, H), dtype=jnp.float32)
        W_gate = jax.random.normal(ks[3], (E, H, D), dtype=jnp.float32) * scale
        b_gate = jnp.zeros((E, H), dtype=jnp.float32)
        W_down = jax.random.normal(ks[4], (E, D, H), dtype=jnp.float32) * scale
        b_down = jnp.zeros((E, D), dtype=jnp.float32)
        return {'x': x, 'opcode_onehot': opcode_onehot, 'W_up': W_up, 'b_up': b_up, 'W_gate': W_gate, 'b_gate': b_gate, 'W_down': W_down, 'b_down': b_down}
    _L1_cond_all = _L1_cond_setup()
    _L1_cond_in = {k: v for k, v in _L1_cond_all.items() if k in ('W_up', 'b_up', 'W_gate', 'b_gate', 'W_down', 'b_down')}
    del _L1_cond_all

    def _L2_cond_setup():
        import jax, jax.numpy as jnp
        import numpy as np
        key = jax.random.key(seed)
        k1, k2, k3, k4, k5 = jax.random.split(key, 5)
        B, N, T, O, G = (32, 64, 256, 256, 8)
        x = jax.random.normal(k1, (B, N, T), dtype=jnp.float32)
        y = jax.random.uniform(k2, (B, G), dtype=jnp.float32)
        weight = jax.random.normal(k3, (G, O, T), dtype=jnp.float32) * (1.0 / np.sqrt(T))
        mask = jax.random.uniform(k4, (O, T), dtype=jnp.float32)
        bias = jax.random.normal(k5, (O,), dtype=jnp.float32)
        return {'x': x, 'y': y, 'weight': weight, 'mask': mask, 'bias': bias}
    _L2_cond_all = _L2_cond_setup()
    _L2_cond_in = {k: v for k, v in _L2_cond_all.items() if k in ('weight', 'mask', 'bias')}
    del _L2_cond_all

    def _L3_cond_setup():
        import jax, jax.numpy as jnp
        import numpy as np
        R = 16
        ALPHA = 32.0
        SCALING = ALPHA / R
        key = jax.random.key(seed)
        ks = jax.random.split(key, 6)
        B, T, C, O, E = (16, 375, 256, 256, 8)
        x = jax.random.normal(ks[0], (B, T, C), dtype=jnp.float32)
        w = jax.random.uniform(ks[1], (B, E), dtype=jnp.float32)
        W_base = jax.random.normal(ks[2], (O, C), dtype=jnp.float32) * 0.02
        b_base = jax.random.normal(ks[3], (O,), dtype=jnp.float32) * 0.02
        As = jax.random.normal(ks[4], (E, R, C), dtype=jnp.float32) * 0.02
        Bs = jax.random.normal(ks[5], (E, O, R), dtype=jnp.float32) * 0.02
        return {'x': x, 'w': w, 'W_base': W_base, 'b_base': b_base, 'As': As, 'Bs': Bs}
    _L3_cond_all = _L3_cond_setup()
    _L3_cond_in = {k: v for k, v in _L3_cond_all.items() if k in ('W_base', 'b_base', 'As', 'Bs')}
    del _L3_cond_all
    return {'x': x, 'cond_8': cond_8, 'L0_cond_skill_gate': _L0_cond_in['skill_gate'], 'L0_cond_skill_up': _L0_cond_in['skill_up'], 'L0_cond_skill_down': _L0_cond_in['skill_down'], 'L0_cond_shared_gate': _L0_cond_in['shared_gate'], 'L0_cond_shared_up': _L0_cond_in['shared_up'], 'L0_cond_shared_down': _L0_cond_in['shared_down'], 'L1_cond_W_up': _L1_cond_in['W_up'], 'L1_cond_b_up': _L1_cond_in['b_up'], 'L1_cond_W_gate': _L1_cond_in['W_gate'], 'L1_cond_b_gate': _L1_cond_in['b_gate'], 'L1_cond_W_down': _L1_cond_in['W_down'], 'L1_cond_b_down': _L1_cond_in['b_down'], 'L2_cond_weight': _L2_cond_in['weight'], 'L2_cond_mask': _L2_cond_in['mask'], 'L2_cond_bias': _L2_cond_in['bias'], 'L3_cond_W_base': _L3_cond_in['W_base'], 'L3_cond_b_base': _L3_cond_in['b_base'], 'L3_cond_As': _L3_cond_in['As'], 'L3_cond_Bs': _L3_cond_in['Bs']}

def reference(x, cond_8, L0_cond_skill_gate, L0_cond_skill_up, L0_cond_skill_down, L0_cond_shared_gate, L0_cond_shared_up, L0_cond_shared_down, L1_cond_W_up, L1_cond_b_up, L1_cond_W_gate, L1_cond_b_gate, L1_cond_W_down, L1_cond_b_down, L2_cond_weight, L2_cond_mask, L2_cond_bias, L3_cond_W_base, L3_cond_b_base, L3_cond_As, L3_cond_Bs):
    import jax
    import jax.numpy as jnp

    def _L0_cond_ref(x, router_logits, skill_gate, skill_up, skill_down, shared_gate, shared_up, shared_down):
        import jax, jax.numpy as jnp
        import numpy as np
        TOP_K = 2
        NUM_MOE_LAYERS = 12

        def _gemma_mlp(x, gate_w, up_w, down_w):
            g = jnp.einsum('bsh,hi->bsi', x, gate_w)
            u = jnp.einsum('bsh,hi->bsi', x, up_w)
            return jnp.einsum('bsi,ih->bsh', jax.nn.gelu(g, approximate=True) * u, down_w)
        B = x.shape[0]
        E = skill_gate.shape[0]
        rw = jax.nn.softmax(router_logits.astype(jnp.float32), axis=-1)
        w, sel = jax.lax.top_k(rw, TOP_K)
        w = w / w.sum(axis=-1, keepdims=True)
        w = w.astype(x.dtype)
        scale = 1.0 / NUM_MOE_LAYERS
        w = scale * w + (1.0 - scale) * jax.lax.stop_gradient(w)
        dense_w = jnp.zeros((B, E), x.dtype).at[jnp.arange(B)[:, None], sel].add(w)

        def step(acc, params):
            g, u, d, we = params
            return (acc + we[:, None, None] * _gemma_mlp(x, g, u, d), None)
        out, _ = jax.lax.scan(step, jnp.zeros_like(x), (skill_gate, skill_up, skill_down, dense_w.T))
        out = out + _gemma_mlp(x, shared_gate, shared_up, shared_down)
        return out

    def _L1_cond_ref(x, opcode_onehot, W_up, b_up, W_gate, b_gate, W_down, b_down):
        import jax, jax.numpy as jnp
        import numpy as np
        B, S, D = (16, 512, 256)
        E, H = (8, 512)
        expert = jnp.argmax(opcode_onehot, axis=-1)
        wu, bu = (W_up[expert], b_up[expert])
        wg, bg = (W_gate[expert], b_gate[expert])
        wd, bd = (W_down[expert], b_down[expert])
        up = jnp.einsum('bsd,bhd->bsh', x, wu) + bu[:, None, :]
        gate = jnp.einsum('bsd,bhd->bsh', x, wg) + bg[:, None, :]
        hidden = jax.nn.silu(up) * gate
        out = jnp.einsum('bsh,bdh->bsd', hidden, wd) + bd[:, None, :]
        return out

    def _L2_cond_ref(x, y, weight, mask, bias):
        import jax, jax.numpy as jnp
        import numpy as np
        masked_w = weight * mask[None, :, :]
        w_bot = jnp.einsum('bg,got->bot', y, masked_w)
        return jnp.einsum('bnt,bot->bno', x, w_bot) + bias

    def _L3_cond_ref(x, w, W_base, b_base, As, Bs):
        import jax, jax.numpy as jnp
        import numpy as np
        R = 16
        ALPHA = 32.0
        SCALING = ALPHA / R
        out = jnp.einsum('btc,oc->bto', x, W_base) + b_base
        h = jnp.einsum('btc,erc->bter', x, As)
        lora = jnp.einsum('bter,eor,be->bto', h, Bs, w)
        return out + lora * SCALING
    x = x + _L0_cond_ref(x, cond_8, L0_cond_skill_gate, L0_cond_skill_up, L0_cond_skill_down, L0_cond_shared_gate, L0_cond_shared_up, L0_cond_shared_down)
    x = x + _L1_cond_ref(x, cond_8, L1_cond_W_up, L1_cond_b_up, L1_cond_W_gate, L1_cond_b_gate, L1_cond_W_down, L1_cond_b_down)
    x = x + _L2_cond_ref(x, cond_8, L2_cond_weight, L2_cond_mask, L2_cond_bias)
    x = x + _L3_cond_ref(x, cond_8, L3_cond_W_base, L3_cond_b_base, L3_cond_As, L3_cond_Bs)
    return x

_drawn_inputs = setup_inputs


def setup_inputs(seed=0):
    import zlib

    import numpy as np

    out = dict(_drawn_inputs(seed))
    spreads = {'L1_cond_b_up': (0.0, 0.8), 'L1_cond_b_gate': (0.0, 0.8), 'L1_cond_b_down': (0.0, 0.1)}
    factors = {'L3_cond_b_base': 6.989}
    for name, (base, spread) in spreads.items():
        noise = np.random.default_rng([zlib.crc32(name.encode()), seed]).standard_normal(out[name].shape)
        drawn = base * np.exp(spread * noise) if base else spread * noise
        out[name] = jnp.asarray(drawn.astype(out[name].dtype))
    for name, factor in factors.items():
        out[name] = (out[name] * factor).astype(out[name].dtype)
    return out
```

```python
import numpy as np
import concourse.bass as bass
from concourse import mybir
from contextlib import ExitStack

F32 = mybir.dt.float32
F32R = mybir.dt.float32r
I32 = mybir.dt.int32
U32 = mybir.dt.uint32
ALU = mybir.AluOpType
ACT = mybir.ActivationFunctionType
AX = mybir.AxisListType

P = 128
B, S, D = 4, 512, 256
E = 8
I0 = 1024
H1 = 512
R = 16
KD = D // P
NQ = S // P
MLP_CHUNKS = I0 // P
CH = 3 * MLP_CHUNKS
C1 = H1 // P
PIECES = CH // 2
RAW_SLOTS = 3
W_SLOTS = 4
KIND = 2 * 3
SCALE = 1.0 / 12
LORA_SCALE = 32.0 / R
GRP = 16

PREP_AT = {1: ("route",), 2: ("cols",), 3: ("x", 1), 4: ("x", 2), 5: ("x", 3), 6: ("turn", 0),
           7: ("turn", 1), 8: ("l2w", 0), 10: ("l2w", 1), 12: ("l3w", 0), 14: ("l3w", 1)}
PREPS = [("x", 0)] + [PREP_AT[i] for i in sorted(PREP_AT)]
L1_AFTER = 5
X2_AT = L1_AFTER + 1
L2_AT = 8
L3_AT = 10
TURN_AT = 17
SPLIT_AHEAD = 2

def first(b):
    return isinstance(b, int) and b == 0

def pairs_before(b):
    return 0 if first(b) else b * (CH + 2 * C1) - C1

def hiddens_before(b):
    return 0 if first(b) else b * (CH + C1) - C1

def splits_done(b, i):
    return b * (CH - 2) + i + 1

def tails_before(b):
    return (b - 1) * 2 + len(PREPS)


def schedule(tail):
    pairs, hiddens = {}, {}
    for i in range(CH):
        pairs["L0", i] = len(pairs)
        hiddens["L0", i] = len(hiddens)
        if TURN_AT <= i < TURN_AT + C1:
            pairs["turn", i - TURN_AT] = len(pairs)
        if tail and i == L1_AFTER:
            for c in range(C1):
                pairs["L1", c] = len(pairs)
                hiddens["L1", c] = len(hiddens)
    return pairs, hiddens


SCHED = {False: schedule(False), True: schedule(True)}
ORDER = {later: list(SCHED[later][0]) for later in SCHED}


def hidden_of(b, i):
    return SCHED[not first(b)][1]["L0", i]


def pair_of(b, what, i):
    return SCHED[not first(b)][0][what, i]


ROUTE_STEPS = 15


def raw_slot(p):
    return (p - 1) % RAW_SLOTS if p else RAW_SLOTS - 1


def raw_uses(b, p):
    s = raw_slot(p)
    per = sum(raw_slot(q) == s for q in range(1, PIECES))
    return per * b + sum(raw_slot(q) == s for q in range(1, p + 1)) + (s == RAW_SLOTS - 1)


def build(nc, t):
    ctx = ExitStack()
    with ctx:
        def sb(name, shape, dt=F32):
            return ctx.enter_context(nc.sbuf_tensor(name, shape, dt))

        def sem(name):
            return ctx.enter_context(nc.semaphore(name))

        raw = sb("raw", [P, RAW_SLOTS, KIND, 2 * P])
        w_hi = sb("w_hi", [P, W_SLOTS, KIND, P], F32R)
        w_lo = sb("w_lo", [P, W_SLOTS, KIND, P], F32R)
        res_hi = sb("res_hi", [P, 2, KIND, P], F32R)
        res_lo = sb("res_lo", [P, 2, KIND, P], F32R)
        early = sb("early", [P, B * NQ * D])
        x_nat = early[:, :].rearrange("p (b q d) -> p b q d", b=B, q=NQ)
        w2_raw = early[:, :].rearrange("p (r d) -> p r d", r=GRP)
        x_hi = sb("x_hi", [P, KD, B * S], F32R)
        x_lo = sb("x_lo", [P, KD, B * S], F32R)
        xs = sb("xs", [P, KD, S])
        xs_hi = sb("xs_hi", [P, KD, S], F32R)
        xs_lo = sb("xs_lo", [P, KD, S], F32R)
        hid = sb("hid", [P, 2, S])
        hid_hi = sb("hid_hi", [P, 2, S], F32R)
        hid_lo = sb("hid_lo", [P, 2, S], F32R)
        raw_up1 = sb("raw_up1", [P, C1, D])
        raw_gate1 = sb("raw_gate1", [P, C1, D])
        raw_down1 = sb("raw_down1", [P, KD, H1])
        w1_hi = sb("w1_hi", [P, C1, KIND, P], F32R)
        w1_lo = sb("w1_lo", [P, C1, KIND, P], F32R)
        w2_all = sb("w2_all", [P, B, KD, D])
        w3_all = sb("w3_all", [P, B, KD, D])
        w2_hi = sb("w2_hi", [P, KD, D], F32R)
        w2_lo = sb("w2_lo", [P, KD, D], F32R)
        w3_hi = sb("w3_hi", [P, KD, D], F32R)
        w3_lo = sb("w3_lo", [P, KD, D], F32R)
        mask_nat = raw_gate1[:, 0:KD, :]
        mask_t = sb("mask_t", [P, KD, D])
        base_nat = raw_gate1[:, KD:2 * KD, :]
        base_t = sb("base_t", [P, KD, D])
        a3 = sb("a3", [P, D])
        b3_nat = sb("b3_nat", [P, KD, E, R])
        b3_t = sb("b3_t", [P, D])
        b3_y = raw_up1[:, :, :]
        bias3 = sb("bias3", [P, D])
        bias2 = sb("bias2", [P, KD])
        out_sb = sb("out_sb", [P, NQ, D])
        ident = sb("ident", [P, P])
        ones = sb("ones", [B, P])
        expand = sb("expand", [E, P])
        logits = sb("logits", [B, E])
        iota_i = sb("iota_i", [B, E], I32)
        iota_f = sb("iota_f", [B, E])
        top_l = sb("top_l", [B, 8])
        arg_l = sb("arg_l", [B, 8], U32)
        neg_max = sb("neg_max", [B, 1])
        expo = sb("expo", [B, E])
        zsum = sb("zsum", [B, 1])
        zrec = sb("zrec", [B, 1])
        prob = sb("prob", [B, E])
        top_p = sb("top_p", [B, 8])
        arg_p = sb("arg_p", [B, 8], U32)
        pick = sb("pick", [B, 5])
        wsum = sb("wsum", [B, 1])
        wrec = sb("wrec", [B, 1])
        wnorm = sb("wnorm", [B, 2])
        wpart = sb("wpart", [B, 2])
        onehot = sb("onehot", [B, E])
        pick_diag = sb("pick_diag", [B, B, 5])
        picks = sb("picks", [P, B, 5])
        chosen = sb("chosen", [1, B * 3], I32)
        cond_oh_t = sb("cond_oh_t", [E, 2, B])
        y_col = sb("y_col", [P, B])
        y_lora = sb("y_lora", [P, B])
        fold16 = sb("fold16", [P, R])
        y_sel = sb("y_sel", [P, B, R])
        bias1_nat = sb("bias1_nat", [E, 2 * H1 + D])
        bias1_all = sb("bias1_all", [P, B, 2 * C1 + KD])
        bias1 = sb("bias1", [P, 2 * C1 + KD])
        w_route = sb("w_route", [P, 2])

        bank_a = [ctx.enter_context(nc.psum_tensor(f"bank_a{n}", [P, S], F32)) for n in range(2)]
        bank_b = [ctx.enter_context(nc.psum_tensor(f"bank_b{n}", [P, S], F32)) for n in range(2)]
        out0 = [ctx.enter_context(nc.psum_tensor(f"out0_{k}", [P, S], F32)) for k in range(KD)]
        tail = [ctx.enter_context(nc.psum_tensor(f"tail{k}", [P, S], F32)) for k in range(KD)]

        raw_in = [sem(f"raw_in{s}") for s in range(RAW_SLOTS)]
        x_in = [sem(f"x_in{b}") for b in range(B)]
        cond_in = sem("cond_in")
        bias1_in = sem("bias1_in")
        w2_in = sem("w2_in")
        turn_in = sem("turn_in")
        l3_in = sem("l3_in")
        w1_in = sem("w1_in")    
        stored = sem("stored")
        const_pool = sem("const_pool")
        const_dve = sem("const_dve")
        route_step = sem("route_step")
        exp_done = sem("exp_done")
        chosen_ready = sem("chosen_ready")
        prep_step = sem("prep_step")
        split_hi = sem("split_hi")
        split_lo = sem("split_lo")
        a_ready = sem("a_ready")
        b_ready = sem("b_ready")
        act_ready = sem("act_ready")
        hid_ready = sem("hid_ready")
        hid_hi_ready = sem("hid_hi_ready")
        hid_lo_ready = sem("hid_lo_ready")
        down_done = sem("down_done")
        turn_lo = sem("turn_lo")
        turn_hi = sem("turn_hi")
        tail_ready = sem("tail_ready")
        tail_free = sem("tail_free")
        x_hi_ready = sem("x_hi_ready")
        out0_free = sem("out0_free")
        xs_ready = sem("xs_ready")
        xs_hi_ready = sem("xs_hi_ready")
        xs_lo_ready = sem("xs_lo_ready")
        w23_hi_ready = sem("w23_hi_ready")
        w23_lo_ready = sem("w23_lo_ready")
        bias1_staged = sem("bias1_staged")
        w_staged = sem("w_staged")
        out_ready = sem("out_ready")

        block = ctx.enter_context(nc.Block())

        def wait(eng, semaphore, value):
            if not (isinstance(value, int) and value <= 0):
                eng.wait_ge(semaphore, value)

        def batch_cols(b):
            return bass.ds(b * S, S)

        def split_slots(i):
            if i < 2:
                return res_hi[:, i], res_lo[:, i]
            s = (i - 2) % W_SLOTS
            return w_hi[:, s], w_lo[:, s]

        @block.sync
        def _(sp):
            def load_piece(p, after, gate, up, down):
                s, c = raw_slot(p), (2 * p) % MLP_CHUNKS
                if after is not None:
                    sp.wait_ge(split_lo, after)
                cols = slice(c * P, (c + 2) * P)
                for n, w in ((0, gate), (2, up)):
                    sp.dma_start(raw[:, s, n:n + 2, :],
                                 w.rearrange("(k p) i -> p k i", p=P)[:, :, cols]).then_inc(raw_in[s], 16)
                for c2 in range(2):
                    sp.dma_start(raw[:, s, 4:6, c2 * P:(c2 + 1) * P],
                                 down[(c + c2) * P:(c + c2 + 1) * P, :]
                                 .rearrange("p (j d) -> p j d", j=KD)).then_inc(raw_in[s], 16)

            shared = [t["L0_cond_shared_" + n] for n in ("gate", "up", "down")]
            skill = [t["L0_cond_skill_" + n] for n in ("gate", "up", "down")]

            def expert_pieces(b, n):
                e = sp.value_load(chosen[0:1, bass.ds(b * 3 + n, 1)], min_val=0, max_val=E - 1)
                rows = [w[bass.ds(e, 1)].rearrange("a r c -> (a r) c") for w in skill]
                for p in range(4 * (n + 1), 4 * (n + 2)):
                    load_piece(p, splits_done(b, 2 * (p - RAW_SLOTS) + 1), *rows)

            x_rows = t["x"].rearrange("b (p q) d -> b p q d", q=NQ)
            sp.dma_start(x_nat[:, 0], x_rows[0]).then_inc(x_in[0], 16)
            load_piece(0, None, *shared)
            sp.dma_start(logits[:, :], t["cond_8"]).then_inc(cond_in, 16)
            load_piece(1, None, *shared)
            load_piece(2, None, *shared)
            for b in range(1, B):
                sp.dma_start(x_nat[:, b], x_rows[b]).then_inc(x_in[b], 16)
            load_piece(3, splits_done(0, 1), *shared)
            sp.wait_ge(chosen_ready, 1)
            expert_pieces(0, 0)
            expert_pieces(0, 1)
            with sp.Fori(1, B) as b:
                for p in range(1, 4):
                    last = max(q for q in range(1, PIECES) if raw_slot(q) == raw_slot(p))
                    load_piece(p, splits_done(b - 1, 2 * last + 1), *shared)
                expert_pieces(b, 0)
                expert_pieces(b, 1)

        @block.gpsimd
        def _(pool):
            nc.gpsimd.memset(ident[:, :], 0.0).then_inc(const_pool, 1)
            nc.gpsimd.memset(expand[:, :], 1.0).then_inc(const_pool, 1)
            nc.gpsimd.iota(iota_i[:, :], pattern=[[1, E]], base=0, channel_multiplier=0).then_inc(const_pool, 1)
            pool.wait_ge(const_pool, 3)
            nc.gpsimd.affine_select(out=ident[:, :], in_=ident[:, :], compare_op=ALU.not_equal, fill=1.0, base=0,
                                    pattern=[[-1, P]], channel_multiplier=1).then_inc(const_pool, 1)
            nc.gpsimd.affine_select(out=expand[:, :], in_=expand[:, :], compare_op=ALU.is_ge, fill=0.0, base=0,
                                    pattern=[[1, P]], channel_multiplier=-R).then_inc(const_pool, 1)
            pool.wait_ge(const_pool, 5)
            nc.gpsimd.affine_select(out=expand[:, :], in_=expand[:, :], compare_op=ALU.is_ge, fill=0.0, base=R - 1,
                                    pattern=[[-1, P]], channel_multiplier=R).then_inc(const_pool, 1)

            for n, name in enumerate(("b_up", "b_gate", "b_down")):
                width = D if n == 2 else H1
                pool.dma_start(bias1_nat[:, n * H1:n * H1 + width], t["L1_cond_" + name]).then_inc(bias1_in, 16)
            pool.dma_start(mask_nat, t["L2_cond_mask"].rearrange("(k p) d -> p k d", p=P)).then_inc(turn_in, 16)
            pool.dma_start(base_nat, t["L3_cond_W_base"].rearrange("(k p) d -> p k d", p=P)).then_inc(turn_in, 16)
            for k in range(KD):
                pool.dma_start(b3_nat[:, k], t["L3_cond_Bs"][:, k * P:(k + 1) * P, :].rearrange("e o r -> o e r"))\
                    .then_inc(turn_in, 16)
            pool.dma_start(a3[:, :], t["L3_cond_As"].rearrange("e r c -> (e r) c")).then_inc(l3_in, 16)
            pool.dma_start(bias3[:, :], t["L3_cond_b_base"].rearrange("(a n) -> a n", a=1).broadcast_to([P, D]))\
                .then_inc(stored, 16)
            pool.dma_start(bias2[:, :], t["L2_cond_bias"].rearrange("(k p) -> p k", p=P),
                           allow_slow_non_contiguous=True).then_inc(l3_in, 16)
            pool.wait_ge(tail_ready, PREPS.index(("x", B - 1)) + 1)
            pool.dma_start(w2_raw, t["L2_cond_weight"].rearrange("g (o r) d -> (g o) r d", r=GRP)).then_inc(w2_in, 16)

            def load_l1(b):
                e = pool.value_load(chosen[0:1, bass.ds(b * 3 + 2, 1)], min_val=0, max_val=E - 1)
                row = lambda name: t["L1_cond_" + name][bass.ds(e, 1)].rearrange("a r c -> (a r) c")
                pool.dma_start(raw_up1[:, :, :], row("W_up").rearrange("(p c) d -> p c d", c=C1)).then_inc(w1_in, 16)
                pool.dma_start(raw_gate1[:, :, :], row("W_gate").rearrange("(p c) d -> p c d", c=C1)).then_inc(w1_in, 16)
                pool.dma_start(raw_down1[:, :, :], row("W_down").rearrange("(j p) h -> p j h", p=P)).then_inc(w1_in, 16)

            def store(b):
                pool.wait_ge(out_ready, 2 * (b + 1))
                pool.dma_start(t["out"][bass.ds(b, 1)].rearrange("a (p q) d -> p (a q) d", q=NQ),
                               out_sb[:, :, :]).then_inc(stored, 16)

            pool.wait_ge(chosen_ready, 1)
            pool.wait_ge(tail_free, len(PREPS))
            load_l1(0)
            with pool.Fori(1, B) as b:
                store(b - 1)
                pool.wait_ge(turn_hi, 2 * C1 * b)
                pool.wait_ge(turn_lo, C1 * b)
                load_l1(b)
            store(B - 1)
            pool.wait_ge(stored, 16 * (B + 1))

        @block.scalar
        def _(act):
            def split(b, i):
                p = i // 2
                act.wait_ge(raw_in[raw_slot(p)], 64 * raw_uses(b, p))
                if i >= 2:
                    if i - W_SLOTS >= 2:
                        wait(act, down_done, hiddens_before(b) + hidden_of(b, i - W_SLOTS) + 1)
                    elif not first(b):
                        last = max(c for c in range(CH) if c >= 2 and (c - i) % W_SLOTS == 0)
                        act.wait_ge(down_done, hiddens_before(b) - CH + last + 1)
                nc.scalar.activation(split_slots(i)[0], raw[:, raw_slot(p), :, (i % 2) * P:(i % 2 + 1) * P],
                                     ACT.Copy).then_inc(split_hi, 1)

            def activate(b, n, pair, func, bias=None):
                act.wait_ge(a_ready, pairs_before(b) + pair + 1)
                wait(act, hid_lo_ready, hiddens_before(b) + n - 1)
                kw = {} if bias is None else {"bias": bias}
                nc.scalar.activation(hid[:, n % 2], bank_a[pair % 2][:, :], func, **kw).then_inc(act_ready, 1)

            def hidden_hi(b, n):
                act.wait_ge(hid_ready, hiddens_before(b) + n + 1)
                wait(act, down_done, hiddens_before(b) + n - 1)
                nc.scalar.activation(hid_hi[:, n % 2], hid[:, n % 2], ACT.Copy).then_inc(hid_hi_ready, 1)

            def prep_hi(what):
                if what[0] == "x":
                    act.wait_ge(tail_ready, PREPS.index(what) + 1)
                    for k in range(KD):
                        nc.scalar.activation(x_hi[:, k, batch_cols(what[1])], tail[k][:, :], ACT.Copy)\
                            .then_inc(x_hi_ready, 1)

            def turn_chunk_hi(b, c):
                pair = pair_of(b, "turn", c)
                flat = w1_hi[:, c].rearrange("p n m -> p (n m)")
                act.wait_ge(b_ready, pairs_before(b) + pair + 1)
                nc.scalar.activation(flat[:, 0:4 * P], bank_a[pair % 2][:, :], ACT.Copy).then_inc(turn_hi, 1)
                nc.scalar.activation(flat[:, 4 * P:6 * P], bank_b[pair % 2][:, 0:2 * P], ACT.Copy).then_inc(turn_hi, 1)

            def l1_chunks(b, n0, pair0):
                for c in range(C1):
                    if c == 0:
                        act.wait_ge(bias1_staged, b)
                    activate(b, n0 + c, pair0 + c, ACT.Silu, bias1[:, c:c + 1])
                    hidden_hi(b, n0 + c)

            def weights23_hi(b):
                act.wait_ge(tail_free, len(PREPS))
                act.wait_ge(tail_ready, tails_before(b))
                for hi, whole in ((w2_hi, w2_all), (w3_hi, w3_all)):
                    nc.scalar.activation(hi[:, :, :].rearrange("p k d -> p (k d)"),
                                         whole[:, bass.ds(b - 1, 1)].rearrange("p a k d -> p (a k d)"),
                                         ACT.Copy).then_inc(w23_hi_ready, 1)

            def residual_hi(b, stage):
                for k in range(KD):
                    if stage < 2:
                        act.wait_ge(xs_ready, 4 * (b - 1) + 2 * stage + k + 1)
                        nc.scalar.activation(xs_hi[:, k], xs[:, k], ACT.Copy).then_inc(xs_hi_ready, 1)
                    else:
                        act.wait_ge(tail_ready, tails_before(b) + 1)
                        nc.scalar.activation(xs_hi[:, k], tail[k][:, :], ACT.Identity,
                                             bias=bias2[:, k:k + 1]).then_inc(xs_hi_ready, 1)

            def batch(b, with_tail):
                for i in range(CH):
                    n, pair = hidden_of(b, i), pair_of(b, "L0", i)
                    activate(b, n, pair, ACT.Gelu_apprx_tanh)
                    if i + SPLIT_AHEAD < CH:
                        split(b, i + SPLIT_AHEAD)
                    hidden_hi(b, n)
                    if first(b) and i in PREP_AT:
                        prep_hi(PREP_AT[i])
                    if with_tail:
                        if i == 0:
                            residual_hi(b, 0)
                        if i == 2:
                            weights23_hi(b)
                        if i == L1_AFTER:
                            l1_chunks(b, n + 1, pair + 1)
                        if i == X2_AT:
                            residual_hi(b, 1)
                        if i == L2_AT:
                            residual_hi(b, 2)
                    if TURN_AT <= i < TURN_AT + C1:
                        turn_chunk_hi(b, i - TURN_AT)

            act.wait_ge(route_step, 3)
            nc.scalar.activation(expo[:, :], logits[:, :], ACT.Exp, bias=neg_max[:, :],
                                 accum_out=zsum[:, :]).then_inc(exp_done, 1)
            split(0, 0)
            prep_hi(("x", 0))
            split(0, 1)
            batch(0, False)
            with act.Fori(1, B) as b:
                batch(b, True)
            residual_hi(B, 0)
            weights23_hi(B)
            l1_chunks(B, 0, 0)
            residual_hi(B, 1)
            residual_hi(B, 2)

        @block.vector
        def _(dve):
            def split(b, i):
                dve.wait_ge(split_hi, splits_done(b, i))
                hi, lo = split_slots(i)
                nc.vector.tensor_tensor(lo, raw[:, raw_slot(i // 2), :, (i % 2) * P:(i % 2 + 1) * P],
                                        hi.bitcast(F32), ALU.subtract).then_inc(split_lo, 1)

            def hidden(b, n, pair, weight=None, bias=None):
                dve.wait_ge(act_ready, hiddens_before(b) + n + 1)
                dve.wait_ge(b_ready, pairs_before(b) + pair + 1)
                tile, bank = hid[:, n % 2], bank_b[pair % 2][:, :]
                if bias is not None:
                    ins = nc.vector.scalar_tensor_tensor(tile, bank, bias, tile, ALU.add, ALU.mult)
                elif weight is not None:
                    ins = nc.vector.scalar_tensor_tensor(tile, bank, weight, tile, ALU.mult, ALU.mult)
                else:
                    ins = nc.vector.tensor_tensor(tile, bank, tile, ALU.mult)
                ins.then_inc(hid_ready, 1)

            def hidden_lo(b, n):
                dve.wait_ge(hid_hi_ready, hiddens_before(b) + n + 1)
                nc.vector.tensor_tensor(hid_lo[:, n % 2], hid[:, n % 2], hid_hi[:, n % 2].bitcast(F32),
                                        ALU.subtract).then_inc(hid_lo_ready, 1)

            def turn_chunk_lo(b, c):
                pair = pair_of(b, "turn", c)
                hi, lo = (w[:, c].rearrange("p n m -> p (n m)") for w in (w1_hi, w1_lo))
                dve.wait_ge(turn_hi, 2 * C1 * b + 2 * c + 1)
                nc.vector.tensor_tensor(lo[:, 0:4 * P], bank_a[pair % 2][:, :], hi[:, 0:4 * P].bitcast(F32), ALU.subtract)
                dve.wait_ge(turn_hi, 2 * C1 * b + 2 * c + 2)
                nc.vector.tensor_tensor(lo[:, 4 * P:6 * P], bank_b[pair % 2][:, 0:2 * P],
                                        hi[:, 4 * P:6 * P].bitcast(F32), ALU.subtract).then_inc(turn_lo, 1)

            def l1_chunks(b, n0, pair0):
                for c in range(C1):
                    if c == 0:
                        dve.wait_ge(bias1_staged, b)
                    hidden(b, n0 + c, pair0 + c, bias=bias1[:, C1 + c:C1 + c + 1])
                    hidden_lo(b, n0 + c)

            def stage_bias1(b):
                nc.vector.tensor_copy(bias1[:, :], bias1_all[:, bass.ds(b - 1, 1)].rearrange("p a c -> p (a c)"))\
                    .then_inc(bias1_staged, 1)

            def stage_route(b):
                nc.vector.tensor_copy(w_route[:, :], picks[:, bass.ds(b, 1), 0:2].rearrange("p a c -> p (a c)"))\
                    .then_inc(w_staged, 1)

            def weights23_lo(b):
                for n, (hi, lo, whole) in enumerate(((w2_hi, w2_lo, w2_all), (w3_hi, w3_lo, w3_all))):
                    dve.wait_ge(w23_hi_ready, 2 * (b - 1) + n + 1)
                    nc.vector.tensor_tensor(lo[:, :, :].rearrange("p k d -> p (k d)"),
                                            whole[:, bass.ds(b - 1, 1)].rearrange("p a k d -> p (a k d)"),
                                            hi[:, :, :].rearrange("p k d -> p (k d)").bitcast(F32),
                                            ALU.subtract).then_inc(w23_lo_ready, 1)

            def residual_lo(b, stage):
                for k in range(KD):
                    dve.wait_ge(xs_hi_ready, 6 * (b - 1) + 2 * stage + k + 1)
                    hi = xs_hi[:, k].bitcast(F32)
                    if stage < 2:
                        ins = nc.vector.tensor_tensor(xs_lo[:, k], xs[:, k], hi, ALU.subtract)
                    else:
                        ins = nc.vector.scalar_tensor_tensor(xs_lo[:, k], tail[k][:, :], bias2[:, k:k + 1], hi,
                                                             ALU.add, ALU.subtract)
                    ins.then_inc(xs_lo_ready, 1)

            def x1(b):
                dve.wait_ge(down_done, hiddens_before(b))
                for k in range(KD):
                    nc.vector.tensor_tensor(xs[:, k], out0[k][:, :], x_lo[:, k, batch_cols(b - 1)].bitcast(F32),
                                            ALU.add).then_inc(out0_free, 1)
                for k in range(KD):
                    dve.wait_ge(out0_free, 2 * (b - 1) + k + 1)
                    nc.vector.tensor_tensor(xs[:, k], xs[:, k], x_hi[:, k, batch_cols(b - 1)].bitcast(F32),
                                            ALU.add).then_inc(xs_ready, 1)
                residual_lo(b, 0)

            def x2(b, n_last):
                dve.wait_ge(down_done, hiddens_before(b) + n_last + 1)
                for k in range(KD):
                    nc.vector.scalar_tensor_tensor(xs[:, k], tail[k][:, :], bias1[:, 2 * C1 + k:2 * C1 + k + 1],
                                                   xs[:, k], ALU.add, ALU.add).then_inc(xs_ready, 1)
                residual_lo(b, 1)

            def output(b):
                dve.wait_ge(tail_ready, tails_before(b) + 2)
                dve.wait_ge(stored, 16 * b)
                for k in range(KD):
                    nc.vector.tensor_tensor(out_sb[:, 2 * k:2 * k + 2], tail[k][:, :].rearrange("p (q d) -> p q d", q=2),
                                            bias3[:, :].unsqueeze(1).broadcast_to([P, 2, D]), ALU.add).then_inc(out_ready, 1)

            steps = [0]

            def chain(ins):
                steps[0] += 1
                ins.then_inc(prep_step, 1)
                dve.wait_ge(prep_step, steps[0])

            def prep(what):
                use = PREPS.index(what)
                if what[0] != "x":
                    dve.wait_ge(tail_ready, use + 1)
                if what[0] == "x":
                    for k in range(KD):
                        cols = batch_cols(what[1])
                        dve.wait_ge(x_hi_ready, 2 * what[1] + k + 1)
                        ins = nc.vector.tensor_tensor(x_lo[:, k, cols], tail[k][:, :], x_hi[:, k, cols].bitcast(F32),
                                                      ALU.subtract)
                elif what[0] == "route":
                    nc.vector.tensor_copy(chosen[0:1, :].rearrange("p (b n) -> p b n", n=3),
                                          tail[0][0:1, 0:B * 5].rearrange("p (b n) -> p b n", n=5)[:, :, 2:5])\
                        .then_inc(chosen_ready, 1)
                    chain(nc.vector.tensor_copy(picks[:, :, :].rearrange("p b n -> p (b n)"), tail[0][:, 0:B * 5]))
                    stage_route(0)
                    ins = nc.vector.tensor_copy(cond_oh_t[:, :, :].rearrange("e n b -> e (n b)"), tail[1][0:E, 0:2 * B])
                elif what[0] == "cols":
                    nc.vector.tensor_scalar(y_lora[:, :], tail[0][:, 0:B], LORA_SCALE, None, ALU.mult)
                    chain(nc.vector.tensor_copy(y_col[:, :], tail[0][:, 0:B]))
                    nc.vector.tensor_tensor(y_sel[:, :, :], y_col[:, :].unsqueeze(2).broadcast_to([P, B, R]),
                                            fold16[:, :].unsqueeze(1).broadcast_to([P, B, R]), ALU.mult)
                    ins = nc.vector.tensor_copy(bias1_all[:, :, :],
                                                tail[1][:, 0:(2 * C1 + KD) * B].rearrange("p (c b) -> p b c", b=B))
                elif what == ("turn", 0):
                    nc.vector.tensor_copy(mask_t[:, :, :].rearrange("p k d -> p (k d)"), tail[0][:, :])
                    chain(nc.vector.tensor_copy(base_t[:, :, :].rearrange("p k d -> p (k d)"), tail[1][:, :]))
                    for k in range(KD):
                        block_k = base_t[:, k, k * P:(k + 1) * P]
                        ins = nc.vector.tensor_tensor(block_k, block_k, ident[:, :], ALU.add)
                elif what == ("turn", 1):
                    chain(nc.vector.tensor_copy(b3_t[:, :], tail[0][:, 0:D]))
                    for b in range(B):
                        ins = nc.vector.tensor_scalar(b3_y[:, b, :], b3_t[:, :], y_lora[:, b:b + 1], None, ALU.mult)
                elif what[0] == "l2w":
                    k = what[1]
                    for h in range(2):
                        dst = w2_all[:, :, k, :].rearrange("p b (o r) -> p r b o", r=GRP)[:, 8 * h:8 * h + 8]
                        msk = mask_t[:, k, :].rearrange("p (o r) -> p r o", r=GRP)[:, 8 * h:8 * h + 8]
                        ins = nc.vector.tensor_tensor(dst, tail[h][:, :].rearrange("p (r b o) -> p r b o", r=8, b=B),
                                                      msk.unsqueeze(2).broadcast_to([P, 8, B, GRP]), ALU.mult)
                    chain(ins)
                    block_k = w2_all[:, :, k, k * P:(k + 1) * P]
                    ins = nc.vector.tensor_tensor(block_k, block_k, ident[:, :].unsqueeze(1).broadcast_to([P, B, P]),
                                                  ALU.add)
                else:
                    for n in range(2):
                        b = 2 * what[1] + n
                        ins = nc.vector.tensor_tensor(w3_all[:, b].rearrange("p k d -> p (k d)"), tail[n][:, :],
                                                      base_t[:, :, :].rearrange("p k d -> p (k d)"), ALU.add)
                ins.then_inc(tail_free, 1)

            def route():
                def step(ins):
                    route_steps[0] += 1
                    ins.then_inc(route_step, 1)
                    dve.wait_ge(route_step, route_steps[0])

                route_steps = [0]
                dve.wait_ge(cond_in, 16)
                step(nc.vector.max(top_l[:, :], logits[:, :]))
                step(nc.vector.max_index(arg_l[:, :], top_l[:, :], logits[:, :]))
                step(nc.vector.tensor_scalar(neg_max[:, :], top_l[:, 0:1], -1.0, None, ALU.mult))
                dve.wait_ge(exp_done, 1)
                step(nc.vector.reciprocal(zrec[:, :], zsum[:, :]))
                step(nc.vector.tensor_scalar(prob[:, :], expo[:, :], zrec[:, 0:1], None, ALU.mult))
                step(nc.vector.max(top_p[:, :], prob[:, :]))
                step(nc.vector.max_index(arg_p[:, :], top_p[:, :], prob[:, :]))
                step(nc.vector.tensor_tensor(wsum[:, :], top_p[:, 0:1], top_p[:, 1:2], ALU.add))
                step(nc.vector.reciprocal(wrec[:, :], wsum[:, :]))
                step(nc.vector.tensor_scalar(wnorm[:, :], top_p[:, 0:2], wrec[:, 0:1], None, ALU.mult))
                step(nc.vector.tensor_scalar(wpart[:, :], wnorm[:, :], SCALE, None, ALU.mult))
                nc.vector.tensor_copy(pick[:, 2:4], arg_p[:, 0:2])
                nc.vector.tensor_copy(pick[:, 4:5], arg_l[:, 0:1])
                step(nc.vector.scalar_tensor_tensor(pick[:, 0:2], wnorm[:, :], 1.0 - SCALE, wpart[:, :],
                                                    ALU.mult, ALU.add))
                dve.wait_ge(const_pool, 4)
                step(nc.vector.tensor_copy(iota_f[:, :], iota_i[:, :]))
                step(nc.vector.tensor_scalar(onehot[:, :], iota_f[:, :], pick[:, 4:5], None, ALU.is_equal))
                step(nc.vector.tensor_tensor(pick_diag[:, :, :], pick[:, :].unsqueeze(1).broadcast_to([B, B, 5]),
                                             ident[0:B, 0:B].unsqueeze(2).broadcast_to([B, B, 5]), ALU.mult))
                assert route_steps[0] == ROUTE_STEPS

            def batch(b, with_tail):
                for i in range(CH):
                    n, pair = hidden_of(b, i), pair_of(b, "L0", i)
                    if i == MLP_CHUNKS:
                        dve.wait_ge(w_staged, b + 1)
                    m = i // MLP_CHUNKS
                    hidden(b, n, pair, weight=w_route[:, m - 1:m] if m else None)
                    if i + SPLIT_AHEAD < CH:
                        split(b, i + SPLIT_AHEAD)
                    hidden_lo(b, n)
                    if first(b) and i in PREP_AT:
                        prep(PREP_AT[i])
                    if with_tail:
                        if i == 0:
                            x1(b)
                            stage_route(b)
                            stage_bias1(b)
                        if i == 2:
                            weights23_lo(b)
                        if i == L1_AFTER:
                            l1_chunks(b, n + 1, pair + 1)
                        if i == X2_AT:
                            x2(b, hidden_of(b, L1_AFTER) + C1)
                        if i == L2_AT:
                            residual_lo(b, 2)
                        if i == L3_AT:
                            output(b)
                    if TURN_AT <= i < TURN_AT + C1:
                        turn_chunk_lo(b, i - TURN_AT)

            nc.vector.memset(ones[:, :], 1.0).then_inc(const_dve, 1)
            route()
            chain(nc.vector.tensor_reduce(fold16[:, :], ident[:, :].rearrange("p (g o) -> p o g", o=R), AX.X, ALU.add))
            split(0, 0)
            prep(("x", 0))
            split(0, 1)
            batch(0, False)
            with dve.Fori(1, B) as b:
                batch(b, True)
            x1(B)
            stage_bias1(B)
            weights23_lo(B)
            l1_chunks(B, 0, 0)
            x2(B, C1 - 1)
            residual_lo(B, 2)
            output(B)

        @block.tensor
        def _(pe):
            def product(out, w_hi_, w_lo_, v_hi, v_lo, start, stop):
                nc.tensor.matmul(out, w_hi_, v_hi, start=start, stop=False)
                nc.tensor.matmul(out, w_hi_, v_lo, start=False, stop=False)
                return nc.tensor.matmul(out, w_lo_, v_hi, start=False, stop=stop)

            def gate_up(b, pair, weights, v_hi, v_lo):
                hi, lo = weights
                wait_pair_free(b, pair)
                for bank, n, done in ((bank_a, 0, a_ready), (bank_b, 2, b_ready)):
                    for k in range(KD):
                        ins = product(bank[pair % 2][:, :], hi[:, n + k], lo[:, n + k], v_hi(k), v_lo(k), k == 0, k == KD - 1)
                    ins.then_inc(done, 1)

            def down(b, n, weights, banks, start, stop):
                hi, lo = weights
                pe.wait_ge(hid_hi_ready, hiddens_before(b) + n + 1)
                for j in range(KD):
                    nc.tensor.matmul(banks[j][:, :], hi[:, 4 + j], hid_hi[:, n % 2], start=start, stop=False)
                    nc.tensor.matmul(banks[j][:, :], lo[:, 4 + j], hid_hi[:, n % 2], start=False, stop=False)
                pe.wait_ge(hid_lo_ready, hiddens_before(b) + n + 1)
                for j in range(KD):
                    ins = nc.tensor.matmul(banks[j][:, :], hi[:, 4 + j], hid_lo[:, n % 2], start=False, stop=stop)
                ins.then_inc(down_done, 1)

            def turn_chunk(b, c):
                pair = pair_of(b, "turn", c)
                if c == 0:
                    pe.wait_ge(w1_in, 48 * (b + 1))
                wait_pair_free(b, pair)
                for n, w in enumerate((raw_up1, raw_gate1)):
                    for k in range(KD):
                        ins = nc.tensor.transpose(bank_a[pair % 2][:, (2 * n + k) * P:(2 * n + k + 1) * P],
                                                  w[:, c, k * P:(k + 1) * P], ident[:, :])
                ins.then_inc(a_ready, 1)
                for j in range(KD):
                    ins = nc.tensor.transpose(bank_b[pair % 2][:, j * P:(j + 1) * P],
                                              raw_down1[:, j, :].rearrange("p (h c) -> p c h", c=C1)[:, c], ident[:, :])
                ins.then_inc(b_ready, 1)

            def wait_pair_free(b, pair):
                if pair >= 2:
                    what, i = ORDER[not first(b)][pair - 2] if not (isinstance(b, int) and b == B) else ("L1", pair - 2)
                    if what == "turn":
                        pe.wait_ge(turn_lo, C1 * b + i + 1)
                        return
                    n = i if isinstance(b, int) and b == B else SCHED[not first(b)][1][what, i]
                    pe.wait_ge(hid_ready, hiddens_before(b) + n + 1)
                elif not first(b):
                    pe.wait_ge(hid_ready, hiddens_before(b) - 1 + pair)

            def l0_gate_up(b, i):
                if i >= 2 or first(b):
                    pe.wait_ge(split_lo, splits_done(b, i))
                if first(b) and i == 0:
                    pe.wait_ge(tail_free, 1)
                gate_up(b, pair_of(b, "L0", i), split_slots(i),
                        lambda k: x_hi[:, k, batch_cols(b)], lambda k: x_lo[:, k, batch_cols(b)])

            def l0_down(b, i, ahead=None):
                if i == 0 and not first(b):
                    pe.wait_ge(out0_free, 2 * b)
                down(b, hidden_of(b, i), split_slots(i), out0, i == 0, i == CH - 1)

            def last_down(b):
                down(b, -1, split_slots(CH - 1), out0, False, True)

            def l1_gate_up(b, c, pair):
                if c == 0:
                    pe.wait_ge(turn_lo, C1 * b)
                    pe.wait_ge(xs_lo_ready, 6 * (b - 1) + 2)
                gate_up(b, pair, (w1_hi[:, c], w1_lo[:, c]), lambda k: xs_hi[:, k], lambda k: xs_lo[:, k])

            def l1_down(b, c, n):
                down(b, n, (w1_hi[:, c], w1_lo[:, c]), tail, c == 0, c == C1 - 1)

            def l2(b):
                pe.wait_ge(w23_lo_ready, 2 * b)
                pe.wait_ge(xs_lo_ready, 6 * (b - 1) + 4)
                for j in range(KD):
                    for k in range(KD):
                        cols = slice(j * P, (j + 1) * P)
                        ins = product(tail[j][:, :], w2_hi[:, k, cols], w2_lo[:, k, cols],
                                      xs_hi[:, k], xs_lo[:, k], k == 0, k == KD - 1)
                ins.then_inc(tail_ready, 1)

            def l3(b):
                pe.wait_ge(xs_lo_ready, 6 * (b - 1) + 6)
                for q in range(NQ):
                    rows, cols = slice(q * P, (q + 1) * P), slice((q % 2) * D, (q % 2 + 1) * D)
                    for k in range(KD):
                        ins = product(tail[q // 2][:, cols], xs_hi[:, k, rows], xs_lo[:, k, rows],
                                      w3_hi[:, k], w3_lo[:, k], k == 0, k == KD - 1)
                ins.then_inc(tail_ready, 1)

            def prep(what):
                use = PREPS.index(what)
                wait(pe, tail_free, use)
                one = lambda out, lhs, rhs: nc.tensor.matmul(out, lhs, rhs, start=True, stop=True)
                if what[0] == "x":
                    b = what[1]
                    pe.wait_ge(x_in[b], 16)
                    for k in range(KD):
                        for q in range(NQ):
                            ins = nc.tensor.transpose(tail[k][:, q * P:(q + 1) * P], x_nat[:, b, q, k * P:(k + 1) * P],
                                                      ident[:, :])
                elif what[0] == "route":
                    pe.wait_ge(route_step, ROUTE_STEPS)
                    one(tail[0][:, 0:B * 5], ones[:, :], pick_diag[:, :, :].rearrange("p b n -> p (b n)"))
                    one(tail[1][0:E, 0:B], logits[:, :], ident[0:B, 0:B])
                    ins = one(tail[1][0:E, B:2 * B], onehot[:, :], ident[0:B, 0:B])
                elif what[0] == "cols":
                    pe.wait_ge(bias1_in, 48)
                    one(tail[0][:, 0:B], expand[:, :], cond_oh_t[:, 0])
                    for c in range(2 * C1 + KD):
                        if c < 2 * C1:
                            part = bias1_nat[:, (c // C1) * H1:(c // C1 + 1) * H1].rearrange("e (h c) -> e c h", c=C1)[:, c % C1]
                        else:
                            part = bias1_nat[:, 2 * H1 + (c - 2 * C1) * P:2 * H1 + (c - 2 * C1 + 1) * P]
                        ins = one(tail[1][:, c * B:(c + 1) * B], part, cond_oh_t[:, 1])
                elif what == ("turn", 0):
                    pe.wait_ge(turn_in, 64)
                    for bank, w in ((tail[0], mask_nat), (tail[1], base_nat)):
                        for k in range(KD):
                            for j in range(KD):
                                ins = nc.tensor.transpose(bank[:, (k * KD + j) * P:(k * KD + j + 1) * P],
                                                          w[:, j, k * P:(k + 1) * P], ident[:, :])
                elif what == ("turn", 1):
                    for j in range(KD):
                        ins = nc.tensor.transpose(tail[0][:, j * P:(j + 1) * P],
                                                  b3_nat[:, j].rearrange("o e r -> o (e r)"), ident[:, :])
                elif what[0] == "l2w":
                    pe.wait_ge(w2_in, 16)
                    for r in range(GRP):
                        ins = one(tail[r // 8][:, (r % 8) * B * R:(r % 8 + 1) * B * R],
                                  w2_raw[:, r, what[1] * P:(what[1] + 1) * P], y_sel[:, :, :].rearrange("p b o -> p (b o)"))
                else:
                    pe.wait_ge(l3_in, 32)
                    for n in range(2):
                        for k in range(KD):
                            ins = one(tail[n][:, k * D:(k + 1) * D], a3[:, k * P:(k + 1) * P], b3_y[:, 2 * what[1] + n, :])
                ins.then_inc(tail_ready, 1)

            def batch(b, with_tail):
                for i in range(CH):
                    l0_gate_up(b, i)
                    if first(b) and i in PREP_AT:
                        prep(PREP_AT[i])
                    if TURN_AT <= i < TURN_AT + C1:
                        turn_chunk(b, i - TURN_AT)
                    if i == 0:
                        if with_tail:
                            last_down(b)
                    elif with_tail and i == X2_AT:
                        l1_down(b, C1 - 1, hidden_of(b, L1_AFTER) + C1)
                    else:
                        l0_down(b, i - 1)
                    if with_tail:
                        if i == L1_AFTER:
                            n0, pair0 = hidden_of(b, i), pair_of(b, "L0", i)
                            for c in range(C1):
                                l1_gate_up(b, c, pair0 + 1 + c)
                                if c == 0:
                                    l0_down(b, i)
                                else:
                                    l1_down(b, c - 1, n0 + c)
                        if i == L2_AT:
                            l2(b)
                        if i == L3_AT:
                            l3(b)

            pe.wait_ge(const_pool, 6)
            pe.wait_ge(const_dve, 1)
            prep(("x", 0))
            batch(0, False)
            with pe.Fori(1, B) as b:
                batch(b, True)
            last_down(B)
            for c in range(C1):
                l1_gate_up(B, c, c)
                if c:
                    l1_down(B, c - 1, c - 1)
            l1_down(B, C1 - 1, C1 - 1)
            l2(B)
            l3(B)


INPUTS = ["x", "cond_8", "L0_cond_skill_gate", "L0_cond_skill_up", "L0_cond_skill_down", "L0_cond_shared_gate",
          "L0_cond_shared_up", "L0_cond_shared_down", "L1_cond_W_up", "L1_cond_b_up", "L1_cond_W_gate",
          "L1_cond_b_gate", "L1_cond_W_down", "L1_cond_b_down", "L2_cond_weight", "L2_cond_mask", "L2_cond_bias",
          "L3_cond_W_base", "L3_cond_b_base", "L3_cond_As", "L3_cond_Bs"]


def kernel(**inputs):
    import numpy as np
    import concourse.bacc as bacc
    from concourse import mybir
    from concourse.bass_utils import run_bass_kernel_spmd

    nc = bacc.Bacc("TRN2", target_bir_lowering=False, num_devices=1)
    arrays, tensors = {}, {}
    for name in INPUTS:
        a = np.ascontiguousarray(inputs[name])
        arrays[f"in_{name}"] = a
        tensors[name] = nc.dram_tensor(f"in_{name}", a.shape, mybir.dt.from_np(a.dtype), kind="ExternalInput").ap()
    tensors["out"] = nc.dram_tensor("out_x4", (B, S, D), mybir.dt.float32, kind="ExternalOutput").ap()
    build(nc, tensors)
    result = run_bass_kernel_spmd(nc, [arrays], core_ids=[0])
    return result.results[0]["out_x4"]
```

```python
import numpy as np
import concourse.bass as bass
from concourse import mybir
from contextlib import ExitStack

F32 = mybir.dt.float32
F32R = mybir.dt.float32r
I32 = mybir.dt.int32
U32 = mybir.dt.uint32
ALU = mybir.AluOpType
ACT = mybir.ActivationFunctionType
AX = mybir.AxisListType

P = 128
B, S, D = 4, 512, 256
E = 8
I0 = 1024
H1 = 512
R = 16
KD = D // P
NQ = S // P
MLP_CHUNKS = I0 // P
CH = 3 * MLP_CHUNKS
C1 = H1 // P
PIECES = CH // 2
RAW_SLOTS = 3
W_SLOTS = 4
KIND = 2 * 3
SCALE = 1.0 / 12
LORA_SCALE = 32.0 / R
PICK = 5 + E
HALF = S // 2

PREP_AT = {1: ("route",), 2: ("x", 1), 3: ("x", 2), 4: ("x", 3), 5: ("cols",), 6: ("turn",), 8: ("bias",), 9: ("rows",)}
PREPS = [("x", 0)] + [PREP_AT[i] for i in sorted(PREP_AT)]
L1_AFTER = 5
X2_AT = L1_AFTER + 1
OUT_AT = 8
C_AT = 11
A_FROM = 9
A_SPLIT_AT = A_FROM + E + 2
CA_AT = A_SPLIT_AT + 1
XSUM_AT = 22
TURN_AT = 17
SPLIT_AHEAD = 2

def first(b):
    return isinstance(b, int) and b == 0

def pairs_before(b):
    return 0 if first(b) else b * (CH + 2 * C1) - C1

def hiddens_before(b):
    return 0 if first(b) else b * (CH + C1) - C1

def splits_done(b, i):
    return b * (CH - 2) + i + 1

def tails_before(b):
    return b * 3 - 1 + len(PREPS) if not first(b) else len(PREPS)


def schedule(tail):
    pairs, hiddens = {}, {}
    for i in range(CH):
        pairs["L0", i] = len(pairs)
        hiddens["L0", i] = len(hiddens)
        if TURN_AT <= i < TURN_AT + C1:
            pairs["turn", i - TURN_AT] = len(pairs)
        if tail and i == L1_AFTER:
            for c in range(C1):
                pairs["L1", c] = len(pairs)
                hiddens["L1", c] = len(hiddens)
    return pairs, hiddens


SCHED = {False: schedule(False), True: schedule(True)}
ORDER = {later: list(SCHED[later][0]) for later in SCHED}


def hidden_of(b, i):
    return SCHED[not first(b)][1]["L0", i]


def pair_of(b, what, i):
    return SCHED[not first(b)][0][what, i]


ROUTE_STEPS = 15
A_STEPS = E + 3


def product_of(b, what):
    return ("out", "c", "ca").index(what) + 1 - first(b)


def part_of(m, halves):
    return (slice(None), slice(None), slice(m * HALF, (m + 1) * HALF)) if halves else (slice(None), m)


def half_slot(m):
    return slice(None), (m % 4) // 2, slice((m % 2) * HALF, (m % 2 + 1) * HALF)


def last_of_slot(m):
    return m - 3 if m >= 4 else m // 2 - 1


def raw_slot(p):
    return (p - 1) % RAW_SLOTS if p else RAW_SLOTS - 1


def raw_uses(b, p):
    s = raw_slot(p)
    per = sum(raw_slot(q) == s for q in range(1, PIECES))
    return per * b + sum(raw_slot(q) == s for q in range(1, p + 1))


def build(nc, t):
    ctx = ExitStack()
    with ctx:
        def sb(name, shape, dt=F32):
            return ctx.enter_context(nc.sbuf_tensor(name, shape, dt))

        def sem(name):
            return ctx.enter_context(nc.semaphore(name))

        raw = sb("raw", [P, RAW_SLOTS, KIND, 2 * P])
        w_hi = sb("w_hi", [P, W_SLOTS, KIND, P], F32R)
        w_lo = sb("w_lo", [P, W_SLOTS, KIND, P], F32R)
        res_hi = sb("res_hi", [P, 2, KIND, P], F32R)
        res_lo = sb("res_lo", [P, 2, KIND, P], F32R)
        early = sb("early", [P, B * NQ * D])
        x_nat = early[:, :].rearrange("p (b q d) -> p b q d", b=B, q=NQ)
        w2_raw = early[:, :].rearrange("p (g k d) -> p g (k d)", g=E, k=KD)
        x_hi = sb("x_hi", [P, KD, B * S], F32R)
        x_lo = sb("x_lo", [P, KD, B * S], F32R)
        xs = sb("xs", [P, KD, S])
        xs_hi = sb("xs_hi", [P, KD, S], F32R)
        xs_lo = sb("xs_lo", [P, KD, S], F32R)
        hid = sb("hid", [P, 2, S])
        hid_hi = sb("hid_hi", [P, 2, S], F32R)
        hid_lo = sb("hid_lo", [P, 2, S], F32R)
        raw_up1 = sb("raw_up1", [P, C1, D])
        raw_gate1 = sb("raw_gate1", [P, C1, D])
        raw_down1 = sb("raw_down1", [P, KD, H1])
        w1_hi = sb("w1_hi", [P, C1, KIND, P], F32R)
        w1_lo = sb("w1_lo", [P, C1, KIND, P], F32R)
        a2 = sb("a2", [P, KD * D])
        a2_hi = sb("a2_hi", [P, KD * D], F32R)
        a2_lo = sb("a2_lo", [P, KD * D], F32R)
        c3 = sb("c3", [P, KD * D])
        c3_hi = sb("c3_hi", [P, KD * D], F32R)
        c3_lo = sb("c3_lo", [P, KD * D], F32R)
        ca_hi = sb("ca_hi", [P, KD * D], F32R)
        ca_lo = sb("ca_lo", [P, KD * D], F32R)
        mask_nat = sb("mask_nat", [P, KD * D])
        base_nat = raw_gate1[:, 0:KD, :]
        base_t = sb("base_t", [P, KD, D])
        a3 = raw_down1[:, 1, D:2 * D]
        a3_hi = sb("a3_hi", [P, D], F32R)
        a3_lo = sb("a3_lo", [P, D], F32R)
        b3_nat = raw_down1[:, 1, 0:D].rearrange("p (k e r) -> p k e r", k=KD, e=E)
        b3_t = sb("b3_t", [P, D])
        b3_y = raw_up1[:, :, :].rearrange("p b d -> p (b d)")
        b3_y_hi = sb("b3_y_hi", [P, B * D], F32R)
        b3_y_lo = sb("b3_y_lo", [P, B * D], F32R)
        bias2 = sb("bias2", [P, KD])
        bias2_m = sb("bias2_m", [P, KD, B])
        bias2_rows = raw_down1[:, 0, D:2 * D]
        u3 = sb("u3", [P, 1])
        u3_y = sb("u3_y", [P, B])
        u3_work = raw_down1[:, 0, 0:D]
        bias3_b = sb("bias3_b", [B, D])
        bias_row = sb("bias_row", [B, D])
        bias_all = sb("bias_all", [P, B, D])
        out_sb = sb("out_sb", [P, NQ, D])
        bias_diag = out_sb[0:B, :, :]
        ident = sb("ident", [P, P])
        ones = sb("ones", [B, P])
        expand = sb("expand", [E, P])
        logits = sb("logits", [B, E])
        iota_i = sb("iota_i", [B, E], I32)
        iota_f = sb("iota_f", [B, E])
        top_l = sb("top_l", [B, 8])
        arg_l = sb("arg_l", [B, 8], U32)
        neg_max = sb("neg_max", [B, 1])
        expo = sb("expo", [B, E])
        zsum = sb("zsum", [B, 1])
        zrec = sb("zrec", [B, 1])
        prob = sb("prob", [B, E])
        top_p = sb("top_p", [B, 8])
        arg_p = sb("arg_p", [B, 8], U32)
        pick = sb("pick", [B, PICK])
        wsum = sb("wsum", [B, 1])
        wrec = sb("wrec", [B, 1])
        wnorm = sb("wnorm", [B, 2])
        wpart = sb("wpart", [B, 2])
        warm = hid[:, 0, :]
        onehot = sb("onehot", [B, E])
        pick_diag = sb("pick_diag", [B, B, PICK])
        picks = sb("picks", [P, B, PICK])
        chosen = sb("chosen", [1, B * 3], I32)
        cond_oh_t = sb("cond_oh_t", [E, 2, B])
        y_lora = sb("y_lora", [P, B])
        bias1_nat = raw_up1[0:E, :, :].rearrange("e c d -> e (c d)")
        bias1_down = sb("bias1_down", [E, D])
        bias1_all = sb("bias1_all", [P, B, 2 * C1 + KD])
        bias1 = sb("bias1", [P, 2 * C1 + KD])
        mine = sb("mine", [P, PICK])

        bank_a = [ctx.enter_context(nc.psum_tensor(f"bank_a{n}", [P, S], F32)) for n in range(2)]
        bank_b = [ctx.enter_context(nc.psum_tensor(f"bank_b{n}", [P, S], F32)) for n in range(2)]
        out0 = ctx.enter_context(nc.psum_tensor("out0", [P, KD, S], F32))
        tail = ctx.enter_context(nc.psum_tensor("tail", [P, KD, S], F32))

        raw_in = [sem(f"raw_in{s}") for s in range(RAW_SLOTS)]
        first_in = [sem(f"first_in{c}") for c in range(2)]
        x_in = [sem(f"x_in{b}") for b in range(B)]
        cond_in = sem("cond_in")
        bias1_in = sem("bias1_in")
        w2_in = sem("w2_in")
        turn_in = sem("turn_in")
        l3_in = sem("l3_in")
        w1_in = sem("w1_in")    
        rows_moved = sem("rows_moved")
        last_stored = sem("last_stored")
        const_pool = sem("const_pool")
        const_dve = sem("const_dve")
        route_step = sem("route_step")
        exp_done = sem("exp_done")
        chosen_ready = sem("chosen_ready")
        prep_step = sem("prep_step")
        split_hi = sem("split_hi")
        split_lo = sem("split_lo")
        a_ready = sem("a_ready")
        b_ready = sem("b_ready")
        act_ready = sem("act_ready")
        hid_ready = sem("hid_ready")
        hid_hi_ready = sem("hid_hi_ready")
        hid_lo_ready = sem("hid_lo_ready")
        down_done = sem("down_done")
        turn_lo = sem("turn_lo")
        turn_hi = sem("turn_hi")
        tail_ready = sem("tail_ready")
        tail_free = sem("tail_free")
        l3_hi = sem("l3_hi")
        x_hi_ready = sem("x_hi_ready")
        xsum_ready = sem("xsum_ready")
        xs_ready = sem("xs_ready")
        xs_hi_ready = sem("xs_hi_ready")
        xs_lo_ready = sem("xs_lo_ready")
        a2_step = sem("a2_step")
        weights_f = sem("weights_f")
        weights_hi = sem("weights_hi")
        weights_lo = sem("weights_lo")
        bias1_staged = sem("bias1_staged")
        mine_staged = sem("mine_staged")
        out_ready = sem("out_ready")
        warm_ready = sem("warm_ready")

        block = ctx.enter_context(nc.Block())

        def wait(eng, semaphore, value):
            if not (isinstance(value, int) and value <= 0):
                eng.wait_ge(semaphore, value)

        def batch_cols(b):
            return bass.ds(b * S, S)

        def split_slots(i):
            if i < 2:
                return res_hi[:, i], res_lo[:, i]
            s = (i - 2) % W_SLOTS
            return w_hi[:, s], w_lo[:, s]

        @block.sync
        def _(sp):
            def load_piece(p, after, gate, up, down):
                s, c = raw_slot(p), (2 * p) % MLP_CHUNKS
                if after is not None:
                    sp.wait_ge(split_lo, after)
                cols = slice(c * P, (c + 2) * P)
                for n, w in ((0, gate), (2, up)):
                    sp.dma_start(raw[:, s, n:n + 2, :],
                                 w.rearrange("(k p) i -> p k i", p=P)[:, :, cols]).then_inc(raw_in[s], 16)
                for c2 in range(2):
                    sp.dma_start(raw[:, s, 4:6, c2 * P:(c2 + 1) * P],
                                 down[(c + c2) * P:(c + c2 + 1) * P, :]
                                 .rearrange("p (j d) -> p j d", j=KD)).then_inc(raw_in[s], 16)

            shared = [t["L0_cond_shared_" + n] for n in ("gate", "up", "down")]
            skill = [t["L0_cond_skill_" + n] for n in ("gate", "up", "down")]

            def expert_pieces(b, n):
                e = sp.value_load(chosen[0:1, bass.ds(b * 3 + n, 1)], min_val=0, max_val=E - 1)
                rows = [w[bass.ds(e, 1)].rearrange("a r c -> (a r) c") for w in skill]
                for p in range(4 * (n + 1), 4 * (n + 2)):
                    load_piece(p, splits_done(b, 2 * (p - RAW_SLOTS) + 1), *rows)

            x_rows = t["x"].rearrange("b (p q) d -> b p q d", q=NQ)
            for k in range(KD):
                cols = slice(k * P, (k + 1) * P)
                sp.dma_start(x_nat[:, 0, :, cols], x_rows[0][:, :, cols]).then_inc(x_in[0], 16)
            for c in range(2):
                cols = slice(c * P, (c + 1) * P)
                for n, w in ((0, shared[0]), (2, shared[1])):
                    sp.dma_start(raw[:, raw_slot(0), n:n + 2, cols],
                                 w.rearrange("(k p) i -> p k i", p=P)[:, :, cols]).then_inc(first_in[c], 16)
                sp.dma_start(raw[:, raw_slot(0), 4:6, cols], shared[2][cols, :].rearrange("p (j d) -> p j d", j=KD))\
                  .then_inc(first_in[c], 16)
            load_piece(1, None, *shared)
            load_piece(2, None, *shared)
            for b in range(1, B):
                sp.dma_start(x_nat[:, b], x_rows[b]).then_inc(x_in[b], 16)
            load_piece(3, splits_done(0, 1), *shared)
            sp.wait_ge(chosen_ready, 1)
            expert_pieces(0, 0)
            expert_pieces(0, 1)
            with sp.Fori(1, B) as b:
                for p in range(1, 4):
                    last = max(q for q in range(1, PIECES) if raw_slot(q) == raw_slot(p))
                    load_piece(p, splits_done(b - 1, 2 * last + 1), *shared)
                expert_pieces(b, 0)
                expert_pieces(b, 1)
            for h in range(2):
                sp.wait_ge(out_ready, 2 * (B - 1) + h + 1)
                sp.dma_start(t["out"][B - 1].rearrange("(p q) d -> p q d", q=NQ)[:, 2 * h:2 * h + 2],
                             out_sb[:, 2 * h:2 * h + 2, :]).then_inc(last_stored, 16)
            sp.wait_ge(last_stored, 32)

        @block.gpsimd
        def _(pool):
            pool.dma_start(logits[:, :], t["cond_8"]).then_inc(cond_in, 16)
            nc.gpsimd.memset(ident[:, :], 0.0).then_inc(const_pool, 1)
            nc.gpsimd.memset(expand[:, :], 1.0).then_inc(const_pool, 1)
            nc.gpsimd.iota(iota_i[:, :], pattern=[[1, E]], base=0, channel_multiplier=0).then_inc(const_pool, 1)
            pool.wait_ge(const_pool, 3)
            nc.gpsimd.affine_select(out=ident[:, :], in_=ident[:, :], compare_op=ALU.not_equal, fill=1.0, base=0,
                                    pattern=[[-1, P]], channel_multiplier=1).then_inc(const_pool, 1)
            nc.gpsimd.affine_select(out=expand[:, :], in_=expand[:, :], compare_op=ALU.is_ge, fill=0.0, base=0,
                                    pattern=[[1, P]], channel_multiplier=-R).then_inc(const_pool, 1)
            pool.wait_ge(const_pool, 5)
            nc.gpsimd.affine_select(out=expand[:, :], in_=expand[:, :], compare_op=ALU.is_ge, fill=0.0, base=R - 1,
                                    pattern=[[-1, P]], channel_multiplier=R).then_inc(const_pool, 1)

            for place, name in ((bias1_nat[:, 0:H1], "b_up"), (bias1_nat[:, H1:2 * H1], "b_gate"),
                                (bias1_down[:, :], "b_down")):
                pool.dma_start(place, t["L1_cond_" + name]).then_inc(bias1_in, 16)
            pool.dma_start(base_nat, t["L3_cond_W_base"].rearrange("(k p) d -> p k d", p=P)).then_inc(turn_in, 16)
            for k in range(KD):
                pool.dma_start(b3_nat[:, k], t["L3_cond_Bs"][:, k * P:(k + 1) * P, :].rearrange("e o r -> o e r"))\
                    .then_inc(turn_in, 16)
            pool.dma_start(a3, t["L3_cond_As"].rearrange("e r c -> (e r) c")).then_inc(l3_in, 16)
            row = lambda name: t[name].rearrange("(a n) -> a n", a=1)
            pool.dma_start(bias3_b[:, :], row("L3_cond_b_base").broadcast_to([B, D])).then_inc(rows_moved, 16)
            pool.dma_start(bias2_rows, row("L2_cond_bias").broadcast_to([P, D])).then_inc(l3_in, 16)
            pool.dma_start(bias2[:, :], t["L2_cond_bias"].rearrange("(k p) -> p k", p=P),
                           allow_slow_non_contiguous=True).then_inc(l3_in, 16)
            pool.dma_start(mask_nat[:, :].rearrange("p (k d) -> p k d", k=KD),
                           t["L2_cond_mask"].rearrange("(k p) d -> p k d", p=P)).then_inc(w2_in, 16)
            pool.wait_ge(tail_ready, PREPS.index(("x", B - 1)) + 1)
            for k in range(KD):
                pool.dma_start(w2_raw[:, :, k * D:(k + 1) * D],
                               t["L2_cond_weight"][:, k * P:(k + 1) * P, :].rearrange("g p d -> p g d")).then_inc(w2_in, 16)

            def load_l1(b):
                e = pool.value_load(chosen[0:1, bass.ds(b * 3 + 2, 1)], min_val=0, max_val=E - 1)
                row = lambda name: t["L1_cond_" + name][bass.ds(e, 1)].rearrange("a r c -> (a r) c")
                pool.dma_start(raw_up1[:, :, :], row("W_up").rearrange("(p c) d -> p c d", c=C1)).then_inc(w1_in, 16)
                pool.dma_start(raw_gate1[:, :, :], row("W_gate").rearrange("(p c) d -> p c d", c=C1)).then_inc(w1_in, 16)
                pool.dma_start(raw_down1[:, :, :], row("W_down").rearrange("(j p) h -> p j h", p=P)).then_inc(w1_in, 16)

            def store(b):
                pool.wait_ge(out_ready, 2 * (b + 1))
                pool.dma_start(t["out"][bass.ds(b, 1)].rearrange("a (p q) d -> p (a q) d", q=NQ),
                               out_sb[:, :, :]).then_inc(rows_moved, 16)

            pool.wait_ge(chosen_ready, 1)
            pool.wait_ge(tail_free, len(PREPS))
            load_l1(0)
            with pool.Fori(1, B) as b:
                store(b - 1)
                pool.wait_ge(turn_hi, 2 * C1 * b)
                pool.wait_ge(turn_lo, C1 * b)
                load_l1(b)
            pool.wait_ge(rows_moved, 16 * B)

        @block.scalar
        def _(act):
            def split(b, i):
                p = i // 2
                if i < 2:
                    act.wait_ge(first_in[i], 48)
                else:
                    act.wait_ge(raw_in[raw_slot(p)], 64 * raw_uses(b, p))
                if i >= 2:
                    if i - W_SLOTS >= 2:
                        wait(act, down_done, hiddens_before(b) + hidden_of(b, i - W_SLOTS) + 1)
                    elif not first(b):
                        last = max(c for c in range(CH) if c >= 2 and (c - i) % W_SLOTS == 0)
                        act.wait_ge(down_done, hiddens_before(b) - CH + last + 1)
                nc.scalar.activation(split_slots(i)[0], raw[:, raw_slot(p), :, (i % 2) * P:(i % 2 + 1) * P],
                                     ACT.Copy).then_inc(split_hi, 1)

            def activate(b, n, pair, func, bias=None):
                act.wait_ge(a_ready, pairs_before(b) + pair + 1)
                wait(act, hid_lo_ready, hiddens_before(b) + n - 1)
                kw = {} if bias is None else {"bias": bias}
                nc.scalar.activation(hid[:, n % 2], bank_a[pair % 2][:, :], func, **kw).then_inc(act_ready, 1)

            def hidden_hi(b, n):
                act.wait_ge(hid_ready, hiddens_before(b) + n + 1)
                wait(act, down_done, hiddens_before(b) + n - 1)
                nc.scalar.activation(hid_hi[:, n % 2], hid[:, n % 2], ACT.Copy).then_inc(hid_hi_ready, 1)

            def prep_hi(what):
                if what[0] == "x":
                    act.wait_ge(tail_ready, PREPS.index(what) + 1)
                    for k in range(KD):
                        nc.scalar.activation(x_hi[:, k, batch_cols(what[1])], tail[:, k, :], ACT.Copy)\
                            .then_inc(x_hi_ready, 1)
                if what[0] == "bias":
                    act.wait_ge(l3_in, 48)
                    nc.scalar.activation(a3_hi[:, :], a3, ACT.Copy).then_inc(l3_hi, 1)
                    act.wait_ge(tail_free, PREPS.index(("turn",)) + 1)
                    nc.scalar.activation(b3_y_hi[:, :], b3_y, ACT.Copy).then_inc(l3_hi, 1)

            def turn_chunk_hi(b, c):
                pair = pair_of(b, "turn", c)
                flat = w1_hi[:, c].rearrange("p n m -> p (n m)")
                act.wait_ge(b_ready, pairs_before(b) + pair + 1)
                nc.scalar.activation(flat[:, 0:4 * P], bank_a[pair % 2][:, :], ACT.Copy).then_inc(turn_hi, 1)
                nc.scalar.activation(flat[:, 4 * P:6 * P], bank_b[pair % 2][:, 0:2 * P], ACT.Copy).then_inc(turn_hi, 1)

            def l1_chunks(b, n0, pair0):
                for c in range(C1):
                    if c == 0:
                        act.wait_ge(bias1_staged, b)
                    activate(b, n0 + c, pair0 + c, ACT.Silu, bias1[:, c:c + 1])
                    hidden_hi(b, n0 + c)

            def weights_split_hi(hi, whole, ready):
                act.wait_ge(*ready)
                nc.scalar.activation(hi[:, :], whole, ACT.Copy).then_inc(weights_hi, 1)

            def residual_hi(b, stage, halves=False, parts=(0, 1)):
                for m in parts:
                    act.wait_ge(xs_ready, 4 * (b - 1) + 2 * stage + m + 1)
                    part = part_of(m, halves)
                    nc.scalar.activation(xs_hi[part], xs[part], ACT.Copy).then_inc(xs_hi_ready, 1)

            def last_l1():
                for m in range(2 * C1):
                    slot = half_slot(m)
                    act.wait_ge(a_ready, pairs_before(B) + m + 1)
                    act.wait_ge(hid_lo_ready, hiddens_before(B) + last_of_slot(m))
                    nc.scalar.activation(hid[slot], bank_a[m % 2][:, 0:HALF], ACT.Silu,
                                         bias=bias1[:, m % C1:m % C1 + 1]).then_inc(act_ready, 1)
                    act.wait_ge(hid_ready, hiddens_before(B) + m + 1)
                    act.wait_ge(down_done, hiddens_before(B) + last_of_slot(m))
                    nc.scalar.activation(hid_hi[slot], hid[slot], ACT.Copy).then_inc(hid_hi_ready, 1)
                    if m == C1 + 1:
                        residual_hi(B, 1, True, (0,))

            def batch(b, with_tail):
                for i in range(CH):
                    n, pair = hidden_of(b, i), pair_of(b, "L0", i)
                    activate(b, n, pair, ACT.Gelu_apprx_tanh)
                    if i + SPLIT_AHEAD < CH:
                        split(b, i + SPLIT_AHEAD)
                    hidden_hi(b, n)
                    if first(b) and i in PREP_AT:
                        prep_hi(PREP_AT[i])
                    if with_tail:
                        if i == 0:
                            residual_hi(b, 0)
                        if i == L1_AFTER:
                            l1_chunks(b, n + 1, pair + 1)
                        if i == X2_AT:
                            residual_hi(b, 1)
                    if i == C_AT:
                        weights_split_hi(c3_hi, c3[:, :], (weights_f, b + 1))
                    if i == A_SPLIT_AT:
                        weights_split_hi(a2_hi, a2[:, :], (a2_step, A_STEPS * (b + 1)))
                    if i == CA_AT:
                        weights_split_hi(ca_hi, tail[:, 1, :], (tail_ready, tails_before(b) + product_of(b, "ca")))
                    if TURN_AT <= i < TURN_AT + C1:
                        turn_chunk_hi(b, i - TURN_AT)

            act.wait_ge(route_step, 3)
            nc.scalar.activation(expo[:, :], logits[:, :], ACT.Exp, bias=neg_max[:, :],
                                 accum_out=zsum[:, :]).then_inc(exp_done, 1)
            prep_hi(("x", 0))
            split(0, 0)
            split(0, 1)
            batch(0, False)
            with act.Fori(1, B) as b:
                batch(b, True)
            residual_hi(B, 0, halves=True)
            last_l1()
            residual_hi(B, 1, True, (1,))

        @block.vector
        def _(dve):
            def split(b, i):
                dve.wait_ge(split_hi, splits_done(b, i))
                hi, lo = split_slots(i)
                nc.vector.tensor_tensor(lo, raw[:, raw_slot(i // 2), :, (i % 2) * P:(i % 2 + 1) * P],
                                        hi.bitcast(F32), ALU.subtract).then_inc(split_lo, 1)

            def hidden(b, n, pair, weight=None, bias=None):
                dve.wait_ge(act_ready, hiddens_before(b) + n + 1)
                dve.wait_ge(b_ready, pairs_before(b) + pair + 1)
                tile, bank = hid[:, n % 2], bank_b[pair % 2][:, :]
                if bias is not None:
                    ins = nc.vector.scalar_tensor_tensor(tile, bank, bias, tile, ALU.add, ALU.mult)
                elif weight is not None:
                    ins = nc.vector.scalar_tensor_tensor(tile, bank, weight, tile, ALU.mult, ALU.mult)
                else:
                    ins = nc.vector.tensor_tensor(tile, bank, tile, ALU.mult)
                ins.then_inc(hid_ready, 1)

            def hidden_lo(b, n):
                dve.wait_ge(hid_hi_ready, hiddens_before(b) + n + 1)
                nc.vector.tensor_tensor(hid_lo[:, n % 2], hid[:, n % 2], hid_hi[:, n % 2].bitcast(F32),
                                        ALU.subtract).then_inc(hid_lo_ready, 1)

            def turn_chunk_lo(b, c):
                pair = pair_of(b, "turn", c)
                hi, lo = (w[:, c].rearrange("p n m -> p (n m)") for w in (w1_hi, w1_lo))
                dve.wait_ge(turn_hi, 2 * C1 * b + 2 * c + 1)
                nc.vector.tensor_tensor(lo[:, 0:4 * P], bank_a[pair % 2][:, :], hi[:, 0:4 * P].bitcast(F32), ALU.subtract)
                dve.wait_ge(turn_hi, 2 * C1 * b + 2 * c + 2)
                nc.vector.tensor_tensor(lo[:, 4 * P:6 * P], bank_b[pair % 2][:, 0:2 * P],
                                        hi[:, 4 * P:6 * P].bitcast(F32), ALU.subtract).then_inc(turn_lo, 1)

            def l1_chunks(b, n0, pair0):
                for c in range(C1):
                    if c == 0:
                        dve.wait_ge(bias1_staged, b)
                    hidden(b, n0 + c, pair0 + c, bias=bias1[:, C1 + c:C1 + c + 1])
                    hidden_lo(b, n0 + c)

            def stage_bias1(b):
                nc.vector.tensor_copy(bias1[:, :], bias1_all[:, bass.ds(b - 1, 1)].rearrange("p a c -> p (a c)"))\
                    .then_inc(bias1_staged, 1)

            def stage_mine(b):
                nc.vector.tensor_copy(mine[:, :], picks[:, bass.ds(b, 1)].rearrange("p a c -> p (a c)"))\
                    .then_inc(mine_staged, 1)

            def a2_steps(b, i):
                n = i - A_FROM
                wait(dve, a2_step, b * A_STEPS + n)
                if n == 0:
                    dve.wait_ge(w2_in, 48)
                    dve.wait_ge(mine_staged, b + 1)
                    ins = nc.vector.tensor_scalar(a2[:, :], w2_raw[:, 0, :], mine[:, 5:6], None, ALU.mult)
                elif n < E:
                    ins = nc.vector.scalar_tensor_tensor(a2[:, :], w2_raw[:, n, :], mine[:, 5 + n:6 + n], a2[:, :],
                                                         ALU.mult, ALU.add)
                elif n == E:
                    ins = nc.vector.tensor_tensor(a2[:, :], a2[:, :], mask_nat[:, :], ALU.mult)
                else:
                    for k in range(KD):
                        block_k = a2[:, k * D + k * P:k * D + (k + 1) * P]
                        ins = nc.vector.tensor_tensor(block_k, block_k, ident[:, :], ALU.add)
                        if k == 0:
                            ins.then_inc(a2_step, 1)
                ins.then_inc(a2_step, 1)

            def c3_sum(b):
                dve.wait_ge(tail_ready, tails_before(b) + product_of(b, "c"))
                nc.vector.tensor_tensor(c3[:, :], tail[:, 0, :], base_t[:, :, :].rearrange("p k d -> p (k d)"), ALU.add)\
                    .then_inc(weights_f, 1)

            def weights_split_lo(b, n, hi, lo, whole):
                dve.wait_ge(weights_hi, 3 * b + n + 1)
                nc.vector.tensor_tensor(lo[:, :], whole, hi[:, :].bitcast(F32), ALU.subtract).then_inc(weights_lo, 1)

            def residual_lo(b, stage, halves=False, parts=(0, 1)):
                for m in parts:
                    dve.wait_ge(xs_hi_ready, 4 * (b - 1) + 2 * stage + m + 1)
                    part = part_of(m, halves)
                    nc.vector.tensor_tensor(xs_lo[part], xs[part], xs_hi[part].bitcast(F32), ALU.subtract)\
                        .then_inc(xs_lo_ready, 1)

            def x_sum(b):
                for k in range(KD):
                    cols = batch_cols(b)
                    nc.vector.tensor_tensor(xs[:, k], x_lo[:, k, cols].bitcast(F32), x_hi[:, k, cols].bitcast(F32),
                                            ALU.add).then_inc(xsum_ready, 1)

            def x1(b, halves=False):
                dve.wait_ge(down_done, hiddens_before(b))
                dve.wait_ge(xsum_ready, 2 * b)
                for m in range(2):
                    part = part_of(m, halves)
                    nc.vector.tensor_tensor(xs[part], out0[part], xs[part], ALU.add).then_inc(xs_ready, 1)
                residual_lo(b, 0, halves)

            def x2(b, n_last):
                dve.wait_ge(down_done, hiddens_before(b) + n_last + 1)
                for k in range(KD):
                    nc.vector.scalar_tensor_tensor(xs[:, k], tail[:, k, :], bias1[:, 2 * C1 + k:2 * C1 + k + 1],
                                                   xs[:, k], ALU.add, ALU.add).then_inc(xs_ready, 1)
                residual_lo(b, 1)

            def output_rows(b, h, bank):
                row = bias_all[:, bass.ds(b - 1, 1)].broadcast_to([P, 2, D])
                nc.vector.tensor_tensor(out_sb[:, 2 * h:2 * h + 2], bank.rearrange("p (q d) -> p q d", q=2), row,
                                        ALU.add).then_inc(out_ready, 1)

            def output(b):
                dve.wait_ge(tail_ready, tails_before(b) + product_of(b, "out"))
                dve.wait_ge(rows_moved, 16 * b)
                for h in range(2):
                    output_rows(b, h, tail[:, h, :])

            def last_tail():
                dve.wait_ge(bias1_staged, B)
                for m in range(2 * C1):
                    slot, c = half_slot(m), m % C1
                    dve.wait_ge(act_ready, hiddens_before(B) + m + 1)
                    dve.wait_ge(b_ready, pairs_before(B) + m + 1)
                    nc.vector.scalar_tensor_tensor(hid[slot], bank_b[m % 2][:, 0:HALF], bias1[:, C1 + c:C1 + c + 1],
                                                   hid[slot], ALU.add, ALU.mult).then_inc(hid_ready, 1)
                    dve.wait_ge(hid_hi_ready, hiddens_before(B) + m + 1)
                    nc.vector.tensor_tensor(hid_lo[slot], hid[slot], hid_hi[slot].bitcast(F32), ALU.subtract)\
                        .then_inc(hid_lo_ready, 1)
                    if m == C1 + 1:
                        last_x2(0)
                dve.wait_ge(rows_moved, 16 * B)
                last_rows(0)
                last_x2(1)
                last_rows(1)

            def last_x2(h):
                dve.wait_ge(down_done, hiddens_before(B) + (h + 1) * C1)
                cols = slice(h * HALF, (h + 1) * HALF)
                for k in range(KD):
                    ins = nc.vector.scalar_tensor_tensor(xs[:, k, cols], (tail, out0)[h][:, k, cols],
                                                         bias1[:, 2 * C1 + k:2 * C1 + k + 1], xs[:, k, cols],
                                                         ALU.add, ALU.add)
                ins.then_inc(xs_ready, 1)
                residual_lo(B, 1, True, (h,))

            def last_rows(h):
                dve.wait_ge(tail_ready, tails_before(B) + h + 1)
                output_rows(B, h, bank_a[h][:, :])

            steps = [0]

            def chain(ins):
                steps[0] += 1
                ins.then_inc(prep_step, 1)
                dve.wait_ge(prep_step, steps[0])

            def prep(what):
                use = PREPS.index(what)
                if what[0] != "x":
                    dve.wait_ge(tail_ready, use + 1)
                if what[0] == "x":
                    for k in range(KD):
                        cols = batch_cols(what[1])
                        dve.wait_ge(x_hi_ready, 2 * what[1] + k + 1)
                        ins = nc.vector.tensor_tensor(x_lo[:, k, cols], tail[:, k, :], x_hi[:, k, cols].bitcast(F32),
                                                      ALU.subtract)
                elif what[0] == "route":
                    sums = tail[:, 0, 0:B * PICK]
                    nc.vector.tensor_copy(chosen[0:1, :].rearrange("p (b n) -> p b n", n=3),
                                          sums[0:1, :].rearrange("p (b n) -> p b n", n=PICK)[:, :, 2:5])\
                        .then_inc(chosen_ready, 1)
                    chain(nc.vector.tensor_copy(picks[:, :, :].rearrange("p b n -> p (b n)"), sums))
                    stage_mine(0)
                    ins = nc.vector.tensor_copy(cond_oh_t[:, :, :].rearrange("e n b -> e (n b)"), tail[0:E, 1, 0:2 * B])
                elif what[0] == "cols":
                    nc.vector.tensor_scalar(y_lora[:, :], tail[:, 0, 0:B], LORA_SCALE, None, ALU.mult)
                    ins = nc.vector.tensor_copy(bias1_all[:, :, :],
                                                tail[:, 1, 0:(2 * C1 + KD) * B].rearrange("p (c b) -> p b c", b=B))
                elif what[0] == "turn":
                    nc.vector.tensor_copy(b3_t[:, :], tail[:, 0, 0:D])
                    chain(nc.vector.tensor_copy(base_t[:, :, :].rearrange("p k d -> p (k d)"), tail[:, 1, :]))
                    for k in range(KD):
                        block_k = base_t[:, k, k * P:(k + 1) * P]
                        nc.vector.tensor_tensor(block_k, block_k, ident[:, :], ALU.add)
                    for b in range(B):
                        nc.vector.tensor_scalar(b3_y[:, b * D:(b + 1) * D], b3_t[:, :], y_lora[:, b:b + 1], None, ALU.mult)
                    dve.wait_ge(l3_in, 48)
                    chain(nc.vector.tensor_tensor_reduce(out=u3_work, in0=a3, in1=bias2_rows, scale=1.0,
                                                         scalar=0.0, op0=ALU.mult, op1=ALU.add, accum_out=u3[:, :]))
                    nc.vector.tensor_scalar(u3_y[:, :], y_lora[:, :], u3[:, 0:1], None, ALU.mult)
                    ins = nc.vector.tensor_copy(bias2_m[:, :, :], bias2[:, :].unsqueeze(2).broadcast_to([P, KD, B]))
                elif what[0] == "rows":
                    flat = bias_all[:, :, :].rearrange("p b d -> p (b d)")
                    nc.vector.tensor_copy(flat[:, 0:S], tail[:, 0, :])
                    ins = nc.vector.tensor_copy(flat[:, S:2 * S], tail[:, 1, :])
                else:
                    dve.wait_ge(rows_moved, 16)
                    chain(nc.vector.tensor_tensor(bias_row[:, :], tail[0:B, 0, 0:D], bias3_b[:, :], ALU.add))
                    nc.vector.tensor_tensor(bias_diag, bias_row[:, :].unsqueeze(1).broadcast_to([B, B, D]),
                                            ident[0:B, 0:B].unsqueeze(2).broadcast_to([B, B, D]), ALU.mult)
                    dve.wait_ge(l3_hi, 1)
                    nc.vector.tensor_tensor(a3_lo[:, :], a3, a3_hi[:, :].bitcast(F32), ALU.subtract)
                    dve.wait_ge(l3_hi, 2)
                    ins = nc.vector.tensor_tensor(b3_y_lo[:, :], b3_y, b3_y_hi[:, :].bitcast(F32), ALU.subtract)
                ins.then_inc(tail_free, 1)

            route_steps = [0]

            def step(ins):
                route_steps[0] += 1
                ins.then_inc(route_step, 1)
                dve.wait_ge(route_step, route_steps[0])

            def route_maximum():
                dve.wait_ge(cond_in, 16)
                step(nc.vector.max(top_l[:, :], logits[:, :]))
                step(nc.vector.max_index(arg_l[:, :], top_l[:, :], logits[:, :]))
                step(nc.vector.tensor_scalar(neg_max[:, :], top_l[:, 0:1], -1.0, None, ALU.mult))

            def route_shares():
                dve.wait_ge(exp_done, 1)
                step(nc.vector.reciprocal(zrec[:, :], zsum[:, :]))
                step(nc.vector.tensor_scalar(prob[:, :], expo[:, :], zrec[:, 0:1], None, ALU.mult))
                step(nc.vector.max(top_p[:, :], prob[:, :]))
                step(nc.vector.max_index(arg_p[:, :], top_p[:, :], prob[:, :]))
                step(nc.vector.tensor_tensor(wsum[:, :], top_p[:, 0:1], top_p[:, 1:2], ALU.add))
                step(nc.vector.reciprocal(wrec[:, :], wsum[:, :]))
                step(nc.vector.tensor_scalar(wnorm[:, :], top_p[:, 0:2], wrec[:, 0:1], None, ALU.mult))
                step(nc.vector.tensor_scalar(wpart[:, :], wnorm[:, :], SCALE, None, ALU.mult))
                nc.vector.tensor_copy(pick[:, 2:4], arg_p[:, 0:2])
                nc.vector.tensor_copy(pick[:, 4:5], arg_l[:, 0:1])
                nc.vector.tensor_copy(pick[:, 5:PICK], logits[:, :])
                step(nc.vector.scalar_tensor_tensor(pick[:, 0:2], wnorm[:, :], 1.0 - SCALE, wpart[:, :],
                                                    ALU.mult, ALU.add))
                dve.wait_ge(const_pool, 4)
                step(nc.vector.tensor_copy(iota_f[:, :], iota_i[:, :]))
                step(nc.vector.tensor_scalar(onehot[:, :], iota_f[:, :], pick[:, 4:5], None, ALU.is_equal))
                step(nc.vector.tensor_tensor(pick_diag[:, :, :], pick[:, :].unsqueeze(1).broadcast_to([B, B, PICK]),
                                             ident[0:B, 0:B].unsqueeze(2).broadcast_to([B, B, PICK]), ALU.mult))
                assert route_steps[0] == ROUTE_STEPS

            def batch(b, with_tail):
                for i in range(CH):
                    n, pair = hidden_of(b, i), pair_of(b, "L0", i)
                    if i == MLP_CHUNKS:
                        dve.wait_ge(mine_staged, b + 1)
                    m = i // MLP_CHUNKS
                    hidden(b, n, pair, weight=mine[:, m - 1:m] if m else None)
                    if i + SPLIT_AHEAD < CH:
                        split(b, i + SPLIT_AHEAD)
                    hidden_lo(b, n)
                    if first(b) and i in PREP_AT:
                        prep(PREP_AT[i])
                    if with_tail:
                        if i == 0:
                            x1(b)
                            stage_mine(b)
                            stage_bias1(b)
                        if i == L1_AFTER:
                            l1_chunks(b, n + 1, pair + 1)
                        if i == X2_AT:
                            x2(b, hidden_of(b, L1_AFTER) + C1)
                        if i == OUT_AT:
                            output(b)
                    if i == C_AT:
                        c3_sum(b)
                        weights_split_lo(b, 0, c3_hi, c3_lo, c3[:, :])
                    if A_FROM <= i <= A_FROM + E + 1:
                        a2_steps(b, i)
                    if i == A_SPLIT_AT:
                        weights_split_lo(b, 1, a2_hi, a2_lo, a2[:, :])
                    if i == CA_AT:
                        weights_split_lo(b, 2, ca_hi, ca_lo, tail[:, 1, :])
                    if TURN_AT <= i < TURN_AT + C1:
                        turn_chunk_lo(b, i - TURN_AT)
                    if i == XSUM_AT:
                        x_sum(b)

            nc.vector.memset(warm, 0.0).then_inc(warm_ready, 1)
            nc.vector.memset(ones[:, :], 1.0).then_inc(const_dve, 1)
            route_maximum()
            prep(("x", 0))
            split(0, 0)
            split(0, 1)
            route_shares()
            batch(0, False)
            with dve.Fori(1, B) as b:
                batch(b, True)
            stage_bias1(B)
            x1(B, halves=True)
            last_tail()

        @block.tensor
        def _(pe):
            def product(out, w_hi_, w_lo_, v_hi, v_lo, start, stop):
                nc.tensor.matmul(out, w_hi_, v_hi, start=start, stop=False)
                nc.tensor.matmul(out, w_hi_, v_lo, start=False, stop=False)
                return nc.tensor.matmul(out, w_lo_, v_hi, start=False, stop=stop)

            def gate_up(b, pair, weights, v_hi, v_lo):
                hi, lo = weights
                wait_pair_free(b, pair)
                for bank, n, done in ((bank_a, 0, a_ready), (bank_b, 2, b_ready)):
                    for k in range(KD):
                        ins = product(bank[pair % 2][:, :], hi[:, n + k], lo[:, n + k], v_hi(k), v_lo(k), k == 0, k == KD - 1)
                    ins.then_inc(done, 1)

            def down(b, n, weights, banks, start, stop):
                hi, lo = weights
                pe.wait_ge(hid_hi_ready, hiddens_before(b) + n + 1)
                for j in range(KD):
                    nc.tensor.matmul(banks[:, j, :], hi[:, 4 + j], hid_hi[:, n % 2], start=start, stop=False)
                    nc.tensor.matmul(banks[:, j, :], lo[:, 4 + j], hid_hi[:, n % 2], start=False, stop=False)
                pe.wait_ge(hid_lo_ready, hiddens_before(b) + n + 1)
                for j in range(KD):
                    ins = nc.tensor.matmul(banks[:, j, :], hi[:, 4 + j], hid_lo[:, n % 2], start=False, stop=stop)
                ins.then_inc(down_done, 1)

            def turn_chunk(b, c):
                pair = pair_of(b, "turn", c)
                if c == 0:
                    pe.wait_ge(w1_in, 48 * (b + 1))
                wait_pair_free(b, pair)
                for n, w in enumerate((raw_up1, raw_gate1)):
                    for k in range(KD):
                        ins = nc.tensor.transpose(bank_a[pair % 2][:, (2 * n + k) * P:(2 * n + k + 1) * P],
                                                  w[:, c, k * P:(k + 1) * P], ident[:, :])
                ins.then_inc(a_ready, 1)
                for j in range(KD):
                    ins = nc.tensor.transpose(bank_b[pair % 2][:, j * P:(j + 1) * P],
                                              raw_down1[:, j, :].rearrange("p (h c) -> p c h", c=C1)[:, c], ident[:, :])
                ins.then_inc(b_ready, 1)

            def wait_pair_free(b, pair):
                if pair >= 2:
                    what, i = ORDER[not first(b)][pair - 2]
                    if what == "turn":
                        pe.wait_ge(turn_lo, C1 * b + i + 1)
                    else:
                        pe.wait_ge(hid_ready, hiddens_before(b) + SCHED[not first(b)][1][what, i] + 1)
                elif not first(b):
                    pe.wait_ge(hid_ready, hiddens_before(b) - 1 + pair)

            def l0_gate_up(b, i):
                if i >= 2 or first(b):
                    pe.wait_ge(split_lo, splits_done(b, i))
                if first(b) and i == 0:
                    pe.wait_ge(tail_free, 1)
                gate_up(b, pair_of(b, "L0", i), split_slots(i),
                        lambda k: x_hi[:, k, batch_cols(b)], lambda k: x_lo[:, k, batch_cols(b)])

            def l0_down(b, i):
                if i == 0 and not first(b):
                    pe.wait_ge(xs_ready, 4 * (b - 1) + 2)
                down(b, hidden_of(b, i), split_slots(i), out0, i == 0, i == CH - 1)

            def last_down(b):
                down(b, -1, split_slots(CH - 1), out0, False, True)

            def l1_gate_up(b, c, pair):
                if c == 0:
                    pe.wait_ge(turn_lo, C1 * b)
                    pe.wait_ge(xs_lo_ready, 4 * (b - 1) + 2)
                gate_up(b, pair, (w1_hi[:, c], w1_lo[:, c]), lambda k: xs_hi[:, k], lambda k: xs_lo[:, k])

            def l1_down(b, c, n):
                if c == 0:
                    pe.wait_ge(weights_lo, 3 * b)
                down(b, n, (w1_hi[:, c], w1_lo[:, c]), tail, c == 0, c == C1 - 1)

            def c_product(b):
                if first(b):
                    pe.wait_ge(tail_free, len(PREPS))
                else:
                    pe.wait_ge(out_ready, 2 * b)
                for k in range(KD):
                    rows, cols = slice(k * P, (k + 1) * P), bass.ds(b * D, D)
                    ins = product(tail[:, 0, k * D:(k + 1) * D], a3_hi[:, rows], a3_lo[:, rows],
                                  b3_y_hi[:, cols], b3_y_lo[:, cols], True, True)
                ins.then_inc(tail_ready, 1)

            def ca_product(b):
                pe.wait_ge(weights_lo, 3 * b + 2)
                for j in range(KD):
                    for k in range(KD):
                        rows = slice(k * D + j * P, k * D + (j + 1) * P)
                        cols = slice(k * D, (k + 1) * D)
                        ins = product(tail[:, 1, j * D:(j + 1) * D], a2_hi[:, rows], a2_lo[:, rows],
                                      c3_hi[:, cols], c3_lo[:, cols], k == 0, k == KD - 1)
                ins.then_inc(tail_ready, 1)

            def x4_tiles(tiles, bank_of):
                for q in tiles:
                    rows = slice(q * P, (q + 1) * P)
                    for k in range(KD):
                        cols = slice(k * D, (k + 1) * D)
                        ins = product(bank_of(q), xs_hi[:, k, rows], xs_lo[:, k, rows], ca_hi[:, cols], ca_lo[:, cols],
                                      k == 0, k == KD - 1)
                ins.then_inc(tail_ready, 1)

            def x4(b):
                pe.wait_ge(xs_lo_ready, 4 * (b - 1) + 4)
                x4_tiles(range(NQ), lambda q: tail[:, q // 2, (q % 2) * D:(q % 2 + 1) * D])

            def last_tail():
                def gate_up_half(m):
                    h, c = m // C1, m % C1
                    cols = slice(h * HALF, (h + 1) * HALF)
                    if c == 0:
                        pe.wait_ge(xs_lo_ready, 4 * (B - 1) + h + 1)
                    if m >= 2:
                        pe.wait_ge(hid_ready, hiddens_before(B) + m - 1)
                    else:
                        pe.wait_ge(hid_ready, hiddens_before(B) + m - 1)
                    for bank, n, done in ((bank_a, 0, a_ready), (bank_b, 2, b_ready)):
                        for k in range(KD):
                            ins = product(bank[m % 2][:, 0:HALF], w1_hi[:, c, n + k], w1_lo[:, c, n + k],
                                          xs_hi[:, k, cols], xs_lo[:, k, cols], k == 0, k == KD - 1)
                        ins.then_inc(done, 1)

                def down_half(m):
                    h, c = m // C1, m % C1
                    cols, slot = slice(h * HALF, (h + 1) * HALF), half_slot(m)
                    pe.wait_ge(hid_lo_ready, hiddens_before(B) + m + 1)
                    for j in range(KD):
                        ins = product((tail, out0)[h][:, j, cols], w1_hi[:, c, 4 + j], w1_lo[:, c, 4 + j],
                                      hid_hi[slot], hid_lo[slot], c == 0, c == C1 - 1)
                    ins.then_inc(down_done, 1)

                pe.wait_ge(turn_lo, C1 * B)
                pe.wait_ge(weights_lo, 3 * B)
                gate_up_half(0)
                gate_up_half(1)
                for m in range(2, 2 * C1):
                    gate_up_half(m)
                    down_half(m - 2)
                for h in range(2):
                    if h:
                        down_half(2 * C1 - 2)
                        down_half(2 * C1 - 1)
                    pe.wait_ge(xs_lo_ready, 4 * (B - 1) + 2 + h + 1)
                    pe.wait_ge(hid_ready, hiddens_before(B) + 2 * C1 - 1 + h)
                    x4_tiles((2 * h, 2 * h + 1), lambda q: bank_a[h][:, (q % 2) * D:(q % 2 + 1) * D])

            def prep(what):
                use = PREPS.index(what)
                wait(pe, tail_free, use)
                one = lambda out, lhs, rhs: nc.tensor.matmul(out, lhs, rhs, start=True, stop=True)
                if what[0] == "x":
                    b = what[1]
                    pe.wait_ge(x_in[b], 16 if b else 32)
                    for k in range(KD):
                        for q in range(NQ):
                            ins = nc.tensor.transpose(tail[:, k, q * P:(q + 1) * P], x_nat[:, b, q, k * P:(k + 1) * P],
                                                      ident[:, :])
                elif what[0] == "route":
                    pe.wait_ge(route_step, ROUTE_STEPS)
                    one(tail[:, 0, 0:B * PICK], ones[:, :], pick_diag[:, :, :].rearrange("p b n -> p (b n)"))
                    one(tail[0:E, 1, 0:B], logits[:, :], ident[0:B, 0:B])
                    ins = one(tail[0:E, 1, B:2 * B], onehot[:, :], ident[0:B, 0:B])
                elif what[0] == "cols":
                    pe.wait_ge(bias1_in, 48)
                    one(tail[:, 0, 0:B], expand[:, :], cond_oh_t[:, 0])
                    for c in range(2 * C1 + KD):
                        if c < 2 * C1:
                            part = bias1_nat[:, (c // C1) * H1:(c // C1 + 1) * H1].rearrange("e (h c) -> e c h", c=C1)[:, c % C1]
                        else:
                            part = bias1_down[:, (c - 2 * C1) * P:(c - 2 * C1 + 1) * P]
                        ins = one(tail[:, 1, c * B:(c + 1) * B], part, cond_oh_t[:, 1])
                elif what[0] == "turn":
                    pe.wait_ge(turn_in, 48)
                    for j in range(KD):
                        nc.tensor.transpose(tail[:, 0, j * P:(j + 1) * P], b3_nat[:, j].rearrange("o e r -> o (e r)"),
                                            ident[:, :])
                    for k in range(KD):
                        for j in range(KD):
                            ins = nc.tensor.transpose(tail[:, 1, (k * KD + j) * P:(k * KD + j + 1) * P],
                                                      base_nat[:, j, k * P:(k + 1) * P], ident[:, :])
                elif what[0] == "rows":
                    for n in range(2):
                        ins = one(tail[:, n, :], ones[:, :], bias_diag[:, 2 * n:2 * n + 2].rearrange("p b d -> p (b d)"))
                else:
                    rows = tail[0:B, 0, 0:D]
                    nc.tensor.matmul(rows, u3_y[:, :], b3_t[:, :], start=True, stop=False)
                    for k in range(KD):
                        ins = nc.tensor.matmul(rows, bias2_m[:, k], base_t[:, k], start=False, stop=k == KD - 1)
                ins.then_inc(tail_ready, 1)

            def batch(b, with_tail):
                for i in range(CH):
                    l0_gate_up(b, i)
                    if first(b) and i in PREP_AT:
                        prep(PREP_AT[i])
                    if TURN_AT <= i < TURN_AT + C1:
                        turn_chunk(b, i - TURN_AT)
                    if i == 0:
                        if with_tail:
                            last_down(b)
                    elif with_tail and i == X2_AT:
                        l1_down(b, C1 - 1, hidden_of(b, L1_AFTER) + C1)
                    else:
                        l0_down(b, i - 1)
                    if with_tail:
                        if i == L1_AFTER:
                            n0, pair0 = hidden_of(b, i), pair_of(b, "L0", i)
                            for c in range(C1):
                                l1_gate_up(b, c, pair0 + 1 + c)
                                if c == 0:
                                    l0_down(b, i)
                                else:
                                    l1_down(b, c - 1, n0 + c)
                        if i == OUT_AT:
                            x4(b)
                    if i == C_AT:
                        c_product(b)
                    if i == CA_AT:
                        ca_product(b)

            pe.wait_ge(warm_ready, 1)
            for _ in range(2):
                nc.tensor.matmul(out0[:, 0, :], warm[:, 0:P], warm, start=True, stop=True)
            pe.wait_ge(const_pool, 6)
            pe.wait_ge(const_dve, 1)
            prep(("x", 0))
            batch(0, False)
            with pe.Fori(1, B) as b:
                batch(b, True)
            last_down(B)
            last_tail()


INPUTS = ["x", "cond_8", "L0_cond_skill_gate", "L0_cond_skill_up", "L0_cond_skill_down", "L0_cond_shared_gate",
          "L0_cond_shared_up", "L0_cond_shared_down", "L1_cond_W_up", "L1_cond_b_up", "L1_cond_W_gate",
          "L1_cond_b_gate", "L1_cond_W_down", "L1_cond_b_down", "L2_cond_weight", "L2_cond_mask", "L2_cond_bias",
          "L3_cond_W_base", "L3_cond_b_base", "L3_cond_As", "L3_cond_Bs"]


def kernel(**inputs):
    import numpy as np
    import concourse.bacc as bacc
    from concourse import mybir
    from concourse.bass_utils import run_bass_kernel_spmd

    nc = bacc.Bacc("TRN2", target_bir_lowering=False, num_devices=1)
    arrays, tensors = {}, {}
    for name in INPUTS:
        a = np.ascontiguousarray(inputs[name])
        arrays[f"in_{name}"] = a
        tensors[name] = nc.dram_tensor(f"in_{name}", a.shape, mybir.dt.from_np(a.dtype), kind="ExternalInput").ap()
    tensors["out"] = nc.dram_tensor("out_x4", (B, S, D), mybir.dt.float32, kind="ExternalOutput").ap()
    build(nc, tensors)
    result = run_bass_kernel_spmd(nc, [arrays], core_ids=[0])
    return result.results[0]["out_x4"]
```

```python
import numpy as np
import concourse.bass as bass
from concourse import mybir
from contextlib import ExitStack

F32 = mybir.dt.float32
F32R = mybir.dt.float32r
I32 = mybir.dt.int32
U32 = mybir.dt.uint32
ALU = mybir.AluOpType
ACT = mybir.ActivationFunctionType

P = 128
B, S, D = 4, 512, 256
E = 8
I0 = 1024
H1 = 512
R = 16
KD = D // P
NQ = S // P
MLP_CHUNKS = I0 // P
CH = 3 * MLP_CHUNKS
C1 = H1 // P
PIECES = CH // 2
RAW_SLOTS = 3
W_SLOTS = 4
KIND = 2 * 3
SCALE = 1.0 / 12
LORA_SCALE = 32.0 / R
PICK = 5 + E
HALF = S // 2

PREP_AT = {2: ("route",), 3: ("x", 1), 4: ("x", 2), 5: ("x", 3), 6: ("turn",), 8: ("bias",), 9: ("rows",)}
PREPS = [("x", 0)] + [PREP_AT[i] for i in sorted(PREP_AT)]
L3_OPERAND_AT = 7
L3_LO_AT = 10
L1_AFTER = 5
X2_AT = L1_AFTER + 1
OUT_AT = 8
C_AT = 11
A_FROM = 9
A_SPLIT_AT = A_FROM + E + 2
CA_AT = CH - 1
XSUM_AT = 14
TURN_AT = 15
SPLIT_AHEAD = 2
WARM = (6, 2)

def first(b):
    return isinstance(b, int) and b == 0

def hiddens_before(b):
    return 0 if first(b) else b * (CH + C1) - C1

def splits_done(b, i):
    return b * (CH - 2) + i + 1

def tails_before(b):
    return len(PREPS) if first(b) else len(PREPS) + b * 3 - 1


def hidden_of(b, i):
    return i + (0 if first(b) or i <= L1_AFTER else C1)


def turned(i):
    c, odd = divmod(i - TURN_AT, 2)
    return c if 0 <= c < C1 and not odd else None


ROUTE_STEPS = 13
A_STEPS = E + 3


def product_of(b, what):
    return ("out", "c", "ca").index(what) + 1 - first(b)


def half_slot(m):
    return slice(None), (m % 4) // 2, slice((m % 2) * HALF, (m % 2 + 1) * HALF)


def last_of_slot(m):
    return m - 3 if m >= 4 else m // 2 - 1


def raw_slot(p):
    return (p - 1) % RAW_SLOTS if p else RAW_SLOTS - 1


def raw_uses(b, p):
    s = raw_slot(p)
    per = sum(raw_slot(q) == s for q in range(1, PIECES))
    return per * b + sum(raw_slot(q) == s for q in range(1, p + 1))


def build(nc, t):
    ctx = ExitStack()
    with ctx:
        def sb(name, shape, dt=F32):
            return ctx.enter_context(nc.sbuf_tensor(name, shape, dt))

        def sem(name):
            return ctx.enter_context(nc.semaphore(name))

        raw = sb("raw", [P, RAW_SLOTS, KIND, 2 * P])
        w_hi = sb("w_hi", [P, W_SLOTS, KIND, P], F32R)
        w_lo = sb("w_lo", [P, W_SLOTS, KIND, P], F32R)
        res_hi = sb("res_hi", [P, 2, KIND, P], F32R)
        res_lo = sb("res_lo", [P, 2, KIND, P], F32R)
        early = sb("early", [P, B * NQ * D])
        x_nat = early[:, :].rearrange("p (b q d) -> p b q d", b=B, q=NQ)
        w2_raw = early[:, :].rearrange("p (g k d) -> p g (k d)", g=E, k=KD)
        x_hi = sb("x_hi", [P, KD, B * S], F32R)
        x_lo = sb("x_lo", [P, KD, B * S], F32R)
        xs = sb("xs", [P, KD, S])
        xs_hi = sb("xs_hi", [P, KD, S], F32R)
        xs_lo = sb("xs_lo", [P, KD, S], F32R)
        hid = sb("hid", [P, 2, S])
        hid_hi = sb("hid_hi", [P, 2, S], F32R)
        hid_lo = sb("hid_lo", [P, 2, S], F32R)
        raw_up1 = sb("raw_up1", [P, KD, H1])
        raw_gate1 = sb("raw_gate1", [P, KD, H1])
        raw_down1 = sb("raw_down1", [P, C1, D])
        w1_hi = sb("w1_hi", [P, C1, KIND, P], F32R)
        w1_lo = sb("w1_lo", [P, C1, KIND, P], F32R)
        a2 = sb("a2", [P, KD * D])
        a2_hi = sb("a2_hi", [P, KD * D], F32R)
        a2_lo = sb("a2_lo", [P, KD * D], F32R)
        c3 = sb("c3", [P, KD * D])
        c3_hi = sb("c3_hi", [P, KD * D], F32R)
        c3_lo = sb("c3_lo", [P, KD * D], F32R)
        ca_hi = sb("ca_hi", [P, KD * D], F32R)
        ca_lo = sb("ca_lo", [P, KD * D], F32R)
        mask_nat = sb("mask_nat", [P, KD * D])
        base_nat = raw_gate1[:, 0, :].rearrange("p (k d) -> p k d", k=KD)
        base_t = sb("base_t", [P, KD, D])
        a3 = raw_down1[:, 0, :]
        a3_hi = sb("a3_hi", [P, D], F32R)
        a3_lo = sb("a3_lo", [P, D], F32R)
        b3_nat = raw_down1[:, 1, :].rearrange("p (k e r) -> p k e r", k=KD, e=E)
        b3_t = sb("b3_t", [P, D])
        b3_y = raw_up1[:, :, :].rearrange("p k h -> p (k h)")
        b3_y_hi = sb("b3_y_hi", [P, B * D], F32R)
        b3_y_lo = sb("b3_y_lo", [P, B * D], F32R)
        bias2 = sb("bias2", [P, KD])
        bias2_m = sb("bias2_m", [P, KD, B])
        bias2_rows = raw_down1[:, 2, :]
        u3 = sb("u3", [P, 1])
        u3_y = sb("u3_y", [P, B])
        u3_work = raw_down1[:, 3, :]
        bias3_b = sb("bias3_b", [B, D])
        bias_row = sb("bias_row", [B, D])
        bias_all = sb("bias_all", [P, B, D])
        out_sb = sb("out_sb", [P, NQ, D])
        bias_diag = out_sb[0:B, :, :]
        turned_w = out_sb[:, :, :].rearrange("p q d -> p (q d)")[:, 0:KIND * P]
        ident = sb("ident", [P, P])
        ones = sb("ones", [B, P])
        expand = sb("expand", [E, P])
        logits = sb("logits", [B, E])
        top_l = sb("top_l", [B, 8])
        arg_l = sb("arg_l", [B, 8], U32)
        neg_max = sb("neg_max", [B, 1])
        expo = sb("expo", [B, E])
        zsum = sb("zsum", [B, 1])
        zrec = sb("zrec", [B, 1])
        prob = sb("prob", [B, E])
        top_p = sb("top_p", [B, 8])
        arg_p = sb("arg_p", [B, 8], U32)
        pick = sb("pick", [B, PICK])
        wsum = sb("wsum", [B, 1])
        wrec = sb("wrec", [B, 1])
        wnorm = sb("wnorm", [B, 2])
        wpart = sb("wpart", [B, 2])
        warm = hid[:, 0, 0:P]
        pick_diag = sb("pick_diag", [B, B, PICK])
        picks = sb("picks", [P, B, PICK])
        chosen = sb("chosen", [1, B * 3], I32)
        cond_t = sb("cond_t", [E, B])
        y_lora = sb("y_lora", [P, B])
        bias1_raw = sb("bias1_raw", [P, 2 * C1 + KD])
        bias1 = sb("bias1", [P, 2 * C1 + KD])
        spare = sb("spare", [P, 1])
        mine = sb("mine", [P, PICK])

        bank_a = [ctx.enter_context(nc.psum_tensor(f"bank_a{n}", [P, S], F32)) for n in range(2)]
        bank_b = [ctx.enter_context(nc.psum_tensor(f"bank_b{n}", [P, S], F32)) for n in range(2)]
        out0 = ctx.enter_context(nc.psum_tensor("out0", [P, KD, S], F32))
        tail = ctx.enter_context(nc.psum_tensor("tail", [P, KD, S], F32))

        raw_in = [sem(f"raw_in{s}") for s in range(RAW_SLOTS)]
        first_in = [sem(f"first_in{c}") for c in range(2)]
        first_down_in = [sem(f"first_down_in{c}") for c in range(2)]
        x0_in = [sem(f"x0_in{k}") for k in range(KD)]
        x_in = [None] + [sem(f"x_in{b}") for b in range(1, B)]
        cond_in = sem("cond_in")
        w2_in = sem("w2_in")
        turn_in = sem("turn_in")
        l3_in = sem("l3_in")
        w1_in = sem("w1_in")
        bias1_in = sem("bias1_in")
        rows_moved = sem("rows_moved")
        last_stored = sem("last_stored")
        const_pool = sem("const_pool")
        const_dve = sem("const_dve")
        route_step = sem("route_step")
        exp_done = sem("exp_done")
        chosen_ready = sem("chosen_ready")
        prep_step = sem("prep_step")
        split_hi = sem("split_hi")
        split_lo = sem("split_lo")
        a_ready = sem("a_ready")
        b_ready = sem("b_ready")
        act_ready = sem("act_ready")
        hid_ready = sem("hid_ready")
        hid_hi_ready = sem("hid_hi_ready")
        hid_lo_ready = sem("hid_lo_ready")
        down_done = sem("down_done")
        turn_f = sem("turn_f")
        turn_hi = sem("turn_hi")
        turn_lo = sem("turn_lo")
        tail_ready = sem("tail_ready")
        tail_free = sem("tail_free")
        l3_f = sem("l3_f")
        l3_lo = sem("l3_lo")
        l3_hi = sem("l3_hi")
        x_hi_ready = sem("x_hi_ready")
        xsum_ready = sem("xsum_ready")
        xs_ready = sem("xs_ready")
        xs_hi_ready = sem("xs_hi_ready")
        xs_lo_ready = sem("xs_lo_ready")
        a2_step = sem("a2_step")
        weights_f = sem("weights_f")
        weights_hi = sem("weights_hi")
        weights_lo = sem("weights_lo")
        bias1_staged = sem("bias1_staged")
        mine_staged = sem("mine_staged")
        out_ready = sem("out_ready")
        warm_ready = sem("warm_ready")
        x0_turned = sem("x0_turned")
        first_hi = sem("first_hi")
        first_lo = sem("first_lo")
        bank0_done = sem("bank0_done")
        end_hi = sem("end_hi")
        end_f = sem("end_f")
        end_half1 = sem("end_half1")
        end_lo = sem("end_lo")
        end_rows = sem("end_rows")

        block = ctx.enter_context(nc.Block())

        def wait(eng, semaphore, value):
            if not (isinstance(value, int) and value <= 0):
                eng.wait_ge(semaphore, value)

        def batch_cols(b):
            return bass.ds(b * S, S)

        def split_slots(i):
            if i < 2:
                return res_hi[:, i], res_lo[:, i]
            s = (i - 2) % W_SLOTS
            return w_hi[:, s], w_lo[:, s]

        @block.sync
        def _(sp):
            def load_piece(p, after, gate, up, down):
                s, c = raw_slot(p), (2 * p) % MLP_CHUNKS
                if after is not None:
                    sp.wait_ge(split_lo, after)
                cols = slice(c * P, (c + 2) * P)
                for n, w in ((0, gate), (2, up)):
                    sp.dma_start(raw[:, s, n:n + 2, :],
                                 w.rearrange("(k p) i -> p k i", p=P)[:, :, cols]).then_inc(raw_in[s], 16)
                for c2 in range(2):
                    sp.dma_start(raw[:, s, 4:6, c2 * P:(c2 + 1) * P],
                                 down[(c + c2) * P:(c + c2 + 1) * P, :]
                                 .rearrange("p (j d) -> p j d", j=KD)).then_inc(raw_in[s], 16)

            shared = [t["L0_cond_shared_" + n] for n in ("gate", "up", "down")]
            skill = [t["L0_cond_skill_" + n] for n in ("gate", "up", "down")]

            def expert_pieces(b, n):
                e = sp.value_load(chosen[0:1, bass.ds(b * 3 + n, 1)], min_val=0, max_val=E - 1)
                rows = [w[bass.ds(e, 1)].rearrange("a r c -> (a r) c") for w in skill]
                for p in range(4 * (n + 1), 4 * (n + 2)):
                    if first(b) and n == 1 and p % 4 < 3:
                        load_first_l1(p % 4)
                    load_piece(p, splits_done(b, 2 * (p - RAW_SLOTS) + 1), *rows)

            def load_l1(e, raw1, name):
                w = t["L1_cond_" + name][bass.ds(e, 1)].rearrange("a (n j) (k q i) -> q j (a k) n i", j=32, q=4, i=32)
                for q in range(4):
                    sp.dma_start(raw1[32 * q:32 * (q + 1)].rearrange("j k (n i) -> j k n i", i=32), w[q])\
                        .then_inc(w1_in, 16)

            l1_weights = ((raw_gate1, "W_gate"), (raw_down1, "W_down"), (raw_up1, "W_up"))

            def load_first_l1(n):
                if n == 0:
                    sp.wait_ge(tail_ready, PREPS.index(("turn",)) + 1)
                elif n == 1:
                    sp.wait_ge(tail_free, PREPS.index(("bias",)) + 1)
                else:
                    sp.wait_ge(l3_lo, 1)
                load_l1(sp.value_load(chosen[0:1, 2:3], min_val=0, max_val=E - 1), *l1_weights[n])

            x_rows = t["x"].rearrange("b (p q) d -> b p q d", q=NQ)
            for k in range(KD):
                cols = slice(k * P, (k + 1) * P)
                sp.dma_start(x_nat[:, 0, :, cols], x_rows[0][:, :, cols]).then_inc(x0_in[k], 16)
            for c in range(2):
                cols = slice(c * P, (c + 1) * P)
                for n, w in ((0, shared[0]), (2, shared[1])):
                    sp.dma_start(raw[:, raw_slot(0), n:n + 2, cols],
                                 w.rearrange("(k p) i -> p k i", p=P)[:, :, cols]).then_inc(first_in[c], 16)
                sp.dma_start(raw[:, raw_slot(0), 4:6, cols], shared[2][cols, :].rearrange("p (j d) -> p j d", j=KD))\
                  .then_inc(first_down_in[c], 16)
            load_piece(1, None, *shared)
            load_piece(2, None, *shared)
            for b in range(1, B):
                sp.dma_start(x_nat[:, b], x_rows[b]).then_inc(x_in[b], 16)
            load_piece(3, splits_done(0, 1), *shared)
            sp.wait_ge(chosen_ready, 1)
            expert_pieces(0, 0)
            expert_pieces(0, 1)
            with sp.Fori(1, B) as b:
                for p in range(1, 4):
                    last = max(q for q in range(1, PIECES) if raw_slot(q) == raw_slot(p))
                    load_piece(p, splits_done(b - 1, 2 * last + 1), *shared)
                sp.wait_ge(turn_f, 3 * C1 * b)
                e = sp.value_load(chosen[0:1, bass.ds(b * 3 + 2, 1)], min_val=0, max_val=E - 1)
                for raw1, name in l1_weights:
                    load_l1(e, raw1, name)
                expert_pieces(b, 0)
                expert_pieces(b, 1)
            for h in range(2):
                sp.wait_ge(out_ready, 2 * (B - 1) + 1 + 2 * h)
                sp.dma_start(t["out"][B - 1].rearrange("(p q) d -> p q d", q=NQ)[:, 2 * h:2 * h + 2],
                             out_sb[:, 2 * h:2 * h + 2, :]).then_inc(last_stored, 16)
            sp.wait_ge(last_stored, 32)

        @block.gpsimd
        def _(pool):
            pool.dma_start(logits[:, :], t["cond_8"]).then_inc(cond_in, 16)
            nc.gpsimd.memset(ident[:, :], 0.0).then_inc(const_pool, 1)
            nc.gpsimd.memset(expand[:, :], 1.0).then_inc(const_pool, 1)
            pool.wait_ge(const_pool, 2)
            nc.gpsimd.affine_select(out=ident[:, :], in_=ident[:, :], compare_op=ALU.not_equal, fill=1.0, base=0,
                                    pattern=[[-1, P]], channel_multiplier=1).then_inc(const_pool, 1)
            nc.gpsimd.affine_select(out=expand[:, :], in_=expand[:, :], compare_op=ALU.is_ge, fill=0.0, base=0,
                                    pattern=[[1, P]], channel_multiplier=-R).then_inc(const_pool, 1)
            pool.wait_ge(const_pool, 4)
            nc.gpsimd.affine_select(out=expand[:, :], in_=expand[:, :], compare_op=ALU.is_ge, fill=0.0, base=R - 1,
                                    pattern=[[-1, P]], channel_multiplier=R).then_inc(const_pool, 1)

            pool.dma_start(base_nat, t["L3_cond_W_base"].rearrange("(k p) d -> p k d", p=P)).then_inc(turn_in, 16)
            for k in range(KD):
                pool.dma_start(b3_nat[:, k], t["L3_cond_Bs"][:, k * P:(k + 1) * P, :].rearrange("e o r -> o e r"))\
                    .then_inc(turn_in, 16)
            pool.dma_start(a3, t["L3_cond_As"].rearrange("e r c -> (e r) c")).then_inc(l3_in, 16)
            row = lambda name: t[name].rearrange("(a n) -> a n", a=1)
            pool.dma_start(bias3_b[:, :], row("L3_cond_b_base").broadcast_to([B, D])).then_inc(rows_moved, 16)
            pool.dma_start(bias2_rows, row("L2_cond_bias").broadcast_to([P, D])).then_inc(l3_in, 16)
            pool.dma_start(bias2[:, :], t["L2_cond_bias"].rearrange("(k p) -> p k", p=P),
                           allow_slow_non_contiguous=True).then_inc(l3_in, 16)
            pool.dma_start(mask_nat[:, :].rearrange("p (k d) -> p k d", k=KD),
                           t["L2_cond_mask"].rearrange("(k p) d -> p k d", p=P)).then_inc(w2_in, 16)
            pool.wait_ge(tail_ready, PREPS.index(("x", B - 1)) + 1)
            for k in range(KD):
                pool.dma_start(w2_raw[:, :, k * D:(k + 1) * D],
                               t["L2_cond_weight"][:, k * P:(k + 1) * P, :].rearrange("g p d -> p g d")).then_inc(w2_in, 16)

            def load_biases(b):
                e = pool.value_load(chosen[0:1, bass.ds(b * 3 + 2, 1)], min_val=0, max_val=E - 1)
                for n, name in enumerate(("b_up", "b_gate", "b_down")):
                    width = KD if n == 2 else C1
                    pool.dma_start(bias1_raw[:, n * C1:n * C1 + width], t["L1_cond_" + name][bass.ds(e, 1)]
                                   .rearrange("a (c p) -> p (a c)", p=P), allow_slow_non_contiguous=True)\
                        .then_inc(bias1_in, 16)

            def store(b):
                pool.wait_ge(out_ready, 2 * (b + 1))
                pool.dma_start(t["out"][bass.ds(b, 1)].rearrange("a (p q) d -> p (a q) d", q=NQ),
                               out_sb[:, :, :]).then_inc(rows_moved, 16)

            pool.wait_ge(chosen_ready, 1)
            load_biases(0)
            with pool.Fori(1, B) as b:
                store(b - 1)
                pool.wait_ge(bias1_staged, b)
                load_biases(b)
            pool.wait_ge(rows_moved, 16 * B)

        @block.scalar
        def _(act):
            def split(b, i):
                p = i // 2
                if i < 2:
                    act.wait_ge(first_in[i], 32)
                    act.wait_ge(first_down_in[i], 16)
                else:
                    act.wait_ge(raw_in[raw_slot(p)], 64 * raw_uses(b, p))
                if i >= 2:
                    if i - W_SLOTS >= 2:
                        wait(act, down_done, hiddens_before(b) + hidden_of(b, i - W_SLOTS) + 1)
                    elif not first(b):
                        last = max(c for c in range(CH) if c >= 2 and (c - i) % W_SLOTS == 0)
                        act.wait_ge(down_done, hiddens_before(b) - CH + last + 1)
                nc.scalar.activation(split_slots(i)[0], raw[:, raw_slot(p), :, (i % 2) * P:(i % 2 + 1) * P],
                                     ACT.Copy).then_inc(split_hi, 1)

            def activate(b, n, func, bias=None):
                act.wait_ge(a_ready, hiddens_before(b) + n + 1)
                wait(act, hid_lo_ready, hiddens_before(b) + n - 1)
                kw = {} if bias is None else {"bias": bias}
                nc.scalar.activation(hid[:, n % 2], bank_a[n % 2][:, :], func, **kw).then_inc(act_ready, 1)

            def hidden_hi(b, n):
                act.wait_ge(hid_ready, hiddens_before(b) + n + 1)
                wait(act, down_done, hiddens_before(b) + n - 1)
                nc.scalar.activation(hid_hi[:, n % 2], hid[:, n % 2], ACT.Copy).then_inc(hid_hi_ready, 1)

            def prep_hi(what):
                if what[0] == "x":
                    act.wait_ge(tail_ready, PREPS.index(what) + 1)
                    for k in range(KD):
                        nc.scalar.activation(x_hi[:, k, batch_cols(what[1])], tail[:, k, :], ACT.Copy)\
                            .then_inc(x_hi_ready, 1)
                if what[0] == "bias":
                    act.wait_ge(l3_in, 48)
                    nc.scalar.activation(a3_hi[:, :], a3, ACT.Copy).then_inc(l3_hi, 1)
                    act.wait_ge(l3_f, 1)
                    nc.scalar.activation(b3_y_hi[:, :], b3_y, ACT.Copy).then_inc(l3_hi, 1)

            def turn_chunk_hi(b, c):
                act.wait_ge(turn_f, 3 * (C1 * b + c + 1))
                nc.scalar.activation(w1_hi[:, c].rearrange("p n m -> p (n m)"), turned_w, ACT.Copy).then_inc(turn_hi, 1)

            def l1_chunks(b, n0):
                for c in range(C1):
                    if c == 0:
                        act.wait_ge(bias1_staged, b)
                    activate(b, n0 + c, ACT.Silu, bias1[:, c:c + 1])
                    hidden_hi(b, n0 + c)

            def weights_split_hi(hi, whole, ready):
                act.wait_ge(*ready)
                nc.scalar.activation(hi[:, :], whole, ACT.Copy).then_inc(weights_hi, 1)

            def residual_hi(b, stage):
                for k in range(KD):
                    act.wait_ge(xs_ready, 4 * (b - 1) + 2 * stage + k + 1)
                    nc.scalar.activation(xs_hi[:, k], xs[:, k], ACT.Copy).then_inc(xs_hi_ready, 1)

            def second_half_highs(stage):
                for k in range(KD):
                    act.wait_ge(end_f, KD * (2 * stage + 1) + k + 1)
                    nc.scalar.activation(xs_hi[:, k, HALF:S], xs[:, k, HALF:S], ACT.Copy).then_inc(end_half1, 1)

            def last_l1():
                act.wait_ge(bias1_staged, B)
                nc.scalar.activation(spare[:, :], bias1[:, 0:1], ACT.Silu)
                for m in range(2 * C1):
                    slot = half_slot(m)
                    act.wait_ge(a_ready, hiddens_before(B) + m + 1)
                    act.wait_ge(hid_lo_ready, hiddens_before(B) + last_of_slot(m))
                    nc.scalar.activation(hid[slot], bank_a[m % 2][:, 0:HALF], ACT.Silu,
                                         bias=bias1[:, m % C1:m % C1 + 1]).then_inc(act_ready, 1)
                    if m == 1:
                        second_half_highs(0)
                    act.wait_ge(hid_ready, hiddens_before(B) + m + 1)
                    act.wait_ge(down_done, hiddens_before(B) + last_of_slot(m))
                    nc.scalar.activation(hid_hi[slot], hid[slot], ACT.Copy).then_inc(hid_hi_ready, 1)

            def batch(b, with_tail):
                for i in range(CH):
                    n = hidden_of(b, i)
                    activate(b, n, ACT.Gelu_apprx_tanh)
                    if i + SPLIT_AHEAD < CH:
                        split(b, i + SPLIT_AHEAD)
                    hidden_hi(b, n)
                    if first(b) and i in PREP_AT:
                        prep_hi(PREP_AT[i])
                    if with_tail:
                        if i == 0:
                            residual_hi(b, 0)
                        if i == L1_AFTER:
                            l1_chunks(b, n + 1)
                        if i == X2_AT:
                            residual_hi(b, 1)
                    if i == C_AT:
                        weights_split_hi(c3_hi, c3[:, :], (weights_f, b + 1))
                    if i == CA_AT:
                        weights_split_hi(ca_hi, tail[:, 1, :], (tail_ready, tails_before(b) + product_of(b, "ca")))
                    if i == A_SPLIT_AT:
                        weights_split_hi(a2_hi, a2[:, :], (a2_step, A_STEPS * (b + 1)))
                    if turned(i - 1) is not None:
                        turn_chunk_hi(b, turned(i - 1))

            act.wait_ge(route_step, 3)
            nc.scalar.activation(expo[:, :], logits[:, :], ACT.Exp, bias=neg_max[:, :],
                                 accum_out=zsum[:, :]).then_inc(exp_done, 1)
            def first_x_hi(k, ready):
                act.wait_ge(ready, 1)
                nc.scalar.activation(x_hi[:, k, 0:S], tail[:, k, :], ACT.Copy).then_inc(x_hi_ready, 1)

            act.wait_ge(first_in[0], 32)
            nc.scalar.activation(res_hi[:, 0, 0:4], raw[:, raw_slot(0), 0:4, 0:P], ACT.Copy).then_inc(first_hi, 1)
            first_x_hi(0, x0_turned)
            first_x_hi(1, tail_ready)
            act.wait_ge(first_down_in[0], 16)
            nc.scalar.activation(res_hi[:, 0, 4:6], raw[:, raw_slot(0), 4:6, 0:P], ACT.Copy).then_inc(split_hi, 1)
            split(0, 1)
            batch(0, False)
            with act.Fori(1, B) as b:
                batch(b, True)
            last_l1()
            second_half_highs(1)

        @block.vector
        def _(dve):
            def split(b, i):
                dve.wait_ge(split_hi, splits_done(b, i))
                hi, lo = split_slots(i)
                nc.vector.tensor_tensor(lo, raw[:, raw_slot(i // 2), :, (i % 2) * P:(i % 2 + 1) * P],
                                        hi.bitcast(F32), ALU.subtract).then_inc(split_lo, 1)

            def hidden(b, n, weight=None, bias=None):
                dve.wait_ge(act_ready, hiddens_before(b) + n + 1)
                dve.wait_ge(b_ready, hiddens_before(b) + n + 1)
                tile, bank = hid[:, n % 2], bank_b[n % 2][:, :]
                if bias is not None:
                    ins = nc.vector.scalar_tensor_tensor(tile, bank, bias, tile, ALU.add, ALU.mult)
                elif weight is not None:
                    ins = nc.vector.scalar_tensor_tensor(tile, bank, weight, tile, ALU.mult, ALU.mult)
                else:
                    ins = nc.vector.tensor_tensor(tile, bank, tile, ALU.mult)
                ins.then_inc(hid_ready, 1)

            def hidden_lo(b, n):
                dve.wait_ge(hid_hi_ready, hiddens_before(b) + n + 1)
                nc.vector.tensor_tensor(hid_lo[:, n % 2], hid[:, n % 2], hid_hi[:, n % 2].bitcast(F32),
                                        ALU.subtract).then_inc(hid_lo_ready, 1)

            def turn_chunk(b, c):
                if c == 0:
                    dve.wait_ge(w1_in, 192 * (b + 1))
                    dve.wait_ge(rows_moved, 16 * (b + 1))
                for n, block in enumerate((raw_up1[:, :, c * P:(c + 1) * P], raw_gate1[:, :, c * P:(c + 1) * P],
                                           raw_down1[:, c, :].rearrange("p (k m) -> p k m", k=KD))):
                    place = turned_w[:, 2 * n * P:2 * (n + 1) * P].rearrange("p (k m) -> p k m", k=KD)
                    nc.vector.transpose(place, block).then_inc(turn_f, 1)

            def turn_chunk_lo(b, c):
                dve.wait_ge(turn_f, 3 * (C1 * b + c + 1))
                dve.wait_ge(turn_hi, C1 * b + c + 1)
                hi, lo = (w[:, c].rearrange("p n m -> p (n m)") for w in (w1_hi, w1_lo))
                nc.vector.tensor_tensor(lo, turned_w, hi.bitcast(F32), ALU.subtract).then_inc(turn_lo, 1)

            def l1_chunks(b, n0):
                for c in range(C1):
                    if c == 0:
                        dve.wait_ge(bias1_staged, b)
                    hidden(b, n0 + c, bias=bias1[:, C1 + c:C1 + c + 1])
                    hidden_lo(b, n0 + c)

            def stage_bias1(b):
                dve.wait_ge(bias1_in, 48 * b)
                nc.vector.tensor_copy(bias1[:, :], bias1_raw[:, :]).then_inc(bias1_staged, 1)

            def stage_mine(b):
                nc.vector.tensor_copy(mine[:, :], picks[:, bass.ds(b, 1)].rearrange("p a c -> p (a c)"))\
                    .then_inc(mine_staged, 1)

            def a2_steps(b, i):
                n = i - A_FROM
                wait(dve, a2_step, b * A_STEPS + n)
                if n == 0:
                    dve.wait_ge(w2_in, 48)
                    dve.wait_ge(mine_staged, b + 1)
                    ins = nc.vector.tensor_scalar(a2[:, :], w2_raw[:, 0, :], mine[:, 5:6], None, ALU.mult)
                elif n < E:
                    ins = nc.vector.scalar_tensor_tensor(a2[:, :], w2_raw[:, n, :], mine[:, 5 + n:6 + n], a2[:, :],
                                                         ALU.mult, ALU.add)
                elif n == E:
                    ins = nc.vector.tensor_tensor(a2[:, :], a2[:, :], mask_nat[:, :], ALU.mult)
                else:
                    for k in range(KD):
                        block_k = a2[:, k * D + k * P:k * D + (k + 1) * P]
                        ins = nc.vector.tensor_tensor(block_k, block_k, ident[:, :], ALU.add)
                        if k == 0:
                            ins.then_inc(a2_step, 1)
                ins.then_inc(a2_step, 1)

            def c3_sum(b):
                dve.wait_ge(tail_ready, tails_before(b) + product_of(b, "c"))
                nc.vector.tensor_tensor(c3[:, :], tail[:, 0, :], base_t[:, :, :].rearrange("p k d -> p (k d)"), ALU.add)\
                    .then_inc(weights_f, 1)

            def weights_split_lo(b, n, hi, lo, whole):
                dve.wait_ge(weights_hi, 3 * b + n)
                nc.vector.tensor_tensor(lo[:, :], whole, hi[:, :].bitcast(F32), ALU.subtract).then_inc(weights_lo, 1)

            def residual_lo(b, stage):
                for k in range(KD):
                    dve.wait_ge(xs_hi_ready, 4 * (b - 1) + 2 * stage + k + 1)
                    nc.vector.tensor_tensor(xs_lo[:, k], xs[:, k], xs_hi[:, k].bitcast(F32), ALU.subtract)\
                        .then_inc(xs_lo_ready, 1)

            def x_sum(b):
                for k in range(KD):
                    cols = batch_cols(b)
                    nc.vector.tensor_tensor(xs[:, k], x_lo[:, k, cols].bitcast(F32), x_hi[:, k, cols].bitcast(F32),
                                            ALU.add).then_inc(xsum_ready, 1)

            def x1(b):
                dve.wait_ge(down_done, hiddens_before(b))
                dve.wait_ge(xsum_ready, 2 * b)
                for k in range(KD):
                    nc.vector.tensor_tensor(xs[:, k], out0[:, k, :], xs[:, k], ALU.add).then_inc(xs_ready, 1)
                residual_lo(b, 0)

            def x2(b, n_last):
                dve.wait_ge(down_done, hiddens_before(b) + n_last + 1)
                for k in range(KD):
                    nc.vector.scalar_tensor_tensor(xs[:, k], tail[:, k, :], bias1[:, 2 * C1 + k:2 * C1 + k + 1],
                                                   xs[:, k], ALU.add, ALU.add).then_inc(xs_ready, 1)
                residual_lo(b, 1)

            def output_rows(b, q, tiles, sums):
                row = bias_all[:, bass.ds(b - 1, 1)].broadcast_to([P, tiles, D])
                nc.vector.tensor_tensor(out_sb[:, q:q + tiles], sums.rearrange("p (q d) -> p q d", q=tiles), row,
                                        ALU.add).then_inc(out_ready, 1)

            def output(b):
                dve.wait_ge(tail_ready, tails_before(b) + product_of(b, "out"))
                dve.wait_ge(rows_moved, 16 * b)
                for h in range(2):
                    output_rows(b, 2 * h, 2, tail[:, h, :])

            def half(tensor, k, h):
                return tensor[:, k, h * HALF:(h + 1) * HALF]

            def end_sum(stage, h, k, products, out):
                if stage == 0:
                    return nc.vector.tensor_tensor(out, half(products, k, h), half(xs, k, h), ALU.add)
                return nc.vector.scalar_tensor_tensor(out, half(products, k, h), bias1[:, 2 * C1 + k:2 * C1 + k + 1],
                                                      half(xs, k, h), ALU.add, ALU.add)

            def end_highs(stage, products, done):
                for k in range(KD):
                    dve.wait_ge(*done[k])
                    end_sum(stage, 0, k, products, half(xs_hi, k, 0)).then_inc(end_hi, 1)

            def end_floats(stage, h, products, done=None):
                for k in range(KD):
                    if done:
                        dve.wait_ge(*done[k])
                    end_sum(stage, h, k, products, half(xs, k, h)).then_inc(end_f, 1)

            def end_lows(stage, h):
                for k in range(KD):
                    dve.wait_ge(end_f, KD * (2 * stage + h) + k + 1)
                    if h:
                        dve.wait_ge(end_half1, KD * stage + k + 1)
                    else:
                        dve.wait_ge(end_hi, KD * stage + k + 1)
                    nc.vector.tensor_tensor(half(xs_lo, k, h), half(xs, k, h), half(xs_hi, k, h).bitcast(F32),
                                            ALU.subtract).then_inc(end_lo, 1)

            def last_tail():
                for m in range(2 * C1):
                    slot, c = half_slot(m), m % C1
                    dve.wait_ge(act_ready, hiddens_before(B) + m + 1)
                    dve.wait_ge(b_ready, hiddens_before(B) + m + 1)
                    nc.vector.scalar_tensor_tensor(hid[slot], bank_b[m % 2][:, 0:HALF], bias1[:, C1 + c:C1 + c + 1],
                                                   hid[slot], ALU.add, ALU.mult).then_inc(hid_ready, 1)
                    if m == 0:
                        end_floats(0, 1, out0)
                    if m == 1:
                        end_lows(0, 1)
                    if m == C1 + 1:
                        end_highs(1, tail, ((down_done, hiddens_before(B) + C1),) * 2)
                    if m == C1 + 2:
                        end_lows(1, 0)
                    dve.wait_ge(hid_hi_ready, hiddens_before(B) + m + 1)
                    nc.vector.tensor_tensor(hid_lo[slot], hid[slot], hid_hi[slot].bitcast(F32), ALU.subtract)\
                        .then_inc(hid_lo_ready, 1)
                    if m == C1 + 1:
                        end_floats(1, 0, tail)
                end_floats(1, 1, out0, ((bank0_done, 2), (down_done, hiddens_before(B) + 2 * C1)))
                end_lows(1, 1)
                dve.wait_ge(rows_moved, 16 * B)
                for n, (q, tiles, sums) in enumerate(((0, 2, bank_a[0][:, :]), (2, 1, bank_a[1][:, 0:D]),
                                                      (3, 1, bank_b[1][:, 0:D]))):
                    dve.wait_ge(end_rows, n + 1)
                    output_rows(B, q, tiles, sums)

            steps = [0]

            def chain(ins):
                steps[0] += 1
                ins.then_inc(prep_step, 1)
                dve.wait_ge(prep_step, steps[0])

            def prep(what):
                use = PREPS.index(what)
                if what[0] != "x":
                    dve.wait_ge(tail_ready, use + 1)
                if what[0] == "x":
                    for k in range(KD):
                        cols = batch_cols(what[1])
                        dve.wait_ge(x_hi_ready, 2 * what[1] + k + 1)
                        ins = nc.vector.tensor_tensor(x_lo[:, k, cols], tail[:, k, :], x_hi[:, k, cols].bitcast(F32),
                                                      ALU.subtract)
                elif what[0] == "route":
                    sums = tail[:, 0, 0:B * PICK]
                    nc.vector.tensor_copy(chosen[0:1, :].rearrange("p (b n) -> p b n", n=3),
                                          sums[0:1, :].rearrange("p (b n) -> p b n", n=PICK)[:, :, 2:5])\
                        .then_inc(chosen_ready, 1)
                    chain(nc.vector.tensor_copy(picks[:, :, :].rearrange("p b n -> p (b n)"), sums))
                    stage_mine(0)
                    ins = nc.vector.tensor_copy(cond_t[:, :], tail[0:E, 1, 0:B])
                elif what[0] == "turn":
                    nc.vector.tensor_scalar(y_lora[:, :], tail[:, 0, D:D + B], LORA_SCALE, None, ALU.mult)
                    nc.vector.tensor_copy(b3_t[:, :], tail[:, 0, 0:D])
                    chain(nc.vector.tensor_copy(base_t[:, :, :].rearrange("p k d -> p (k d)"), tail[:, 1, :]))
                    for k in range(KD):
                        block_k = base_t[:, k, k * P:(k + 1) * P]
                        nc.vector.tensor_tensor(block_k, block_k, ident[:, :], ALU.add)
                    dve.wait_ge(l3_in, 48)
                    chain(nc.vector.tensor_tensor_reduce(out=u3_work, in0=a3, in1=bias2_rows, scale=1.0,
                                                         scalar=0.0, op0=ALU.mult, op1=ALU.add, accum_out=u3[:, :]))
                    nc.vector.tensor_scalar(u3_y[:, :], y_lora[:, :], u3[:, 0:1], None, ALU.mult)
                    ins = nc.vector.tensor_copy(bias2_m[:, :, :], bias2[:, :].unsqueeze(2).broadcast_to([P, KD, B]))
                elif what[0] == "rows":
                    flat = bias_all[:, :, :].rearrange("p b d -> p (b d)")
                    nc.vector.tensor_copy(flat[:, 0:S], tail[:, 0, :])
                    ins = nc.vector.tensor_copy(flat[:, S:2 * S], tail[:, 1, :])
                else:
                    dve.wait_ge(rows_moved, 16)
                    chain(nc.vector.tensor_tensor(bias_row[:, :], tail[0:B, 0, 0:D], bias3_b[:, :], ALU.add))
                    nc.vector.tensor_tensor(bias_diag, bias_row[:, :].unsqueeze(1).broadcast_to([B, B, D]),
                                            ident[0:B, 0:B].unsqueeze(2).broadcast_to([B, B, D]), ALU.mult)
                    dve.wait_ge(l3_hi, 1)
                    ins = nc.vector.tensor_tensor(a3_lo[:, :], a3, a3_hi[:, :].bitcast(F32), ALU.subtract)
                ins.then_inc(tail_free, 1)

            def l3_operand():
                for b in range(B):
                    ins = nc.vector.tensor_scalar(b3_y[:, b * D:(b + 1) * D], b3_t[:, :], y_lora[:, b:b + 1], None, ALU.mult)
                ins.then_inc(l3_f, 1)

            def l3_operand_lo():
                dve.wait_ge(l3_hi, 2)
                nc.vector.tensor_tensor(b3_y_lo[:, :], b3_y, b3_y_hi[:, :].bitcast(F32), ALU.subtract).then_inc(l3_lo, 1)

            route_steps = [0]

            def step(ins):
                route_steps[0] += 1
                ins.then_inc(route_step, 1)
                dve.wait_ge(route_step, route_steps[0])

            def route_maximum():
                dve.wait_ge(cond_in, 16)
                step(nc.vector.max(top_l[:, :], logits[:, :]))
                step(nc.vector.max_index(arg_l[:, :], top_l[:, :], logits[:, :]))
                step(nc.vector.tensor_scalar(neg_max[:, :], top_l[:, 0:1], -1.0, None, ALU.mult))

            def route_top2():
                dve.wait_ge(exp_done, 1)
                step(nc.vector.reciprocal(zrec[:, :], zsum[:, :]))
                step(nc.vector.tensor_scalar(prob[:, :], expo[:, :], zrec[:, 0:1], None, ALU.mult))
                step(nc.vector.max(top_p[:, :], prob[:, :]))
                step(nc.vector.max_index(arg_p[:, :], top_p[:, :], prob[:, :]))
                step(nc.vector.tensor_tensor(wsum[:, :], top_p[:, 0:1], top_p[:, 1:2], ALU.add))

            def route_shares():
                step(nc.vector.reciprocal(wrec[:, :], wsum[:, :]))
                step(nc.vector.tensor_scalar(wnorm[:, :], top_p[:, 0:2], wrec[:, 0:1], None, ALU.mult))
                step(nc.vector.tensor_scalar(wpart[:, :], wnorm[:, :], SCALE, None, ALU.mult))
                nc.vector.tensor_copy(pick[:, 2:4], arg_p[:, 0:2])
                nc.vector.tensor_copy(pick[:, 4:5], arg_l[:, 0:1])
                nc.vector.tensor_copy(pick[:, 5:PICK], logits[:, :])
                step(nc.vector.scalar_tensor_tensor(pick[:, 0:2], wnorm[:, :], 1.0 - SCALE, wpart[:, :],
                                                    ALU.mult, ALU.add))
                dve.wait_ge(const_pool, 3)
                step(nc.vector.tensor_tensor(pick_diag[:, :, :], pick[:, :].unsqueeze(1).broadcast_to([B, B, PICK]),
                                             ident[0:B, 0:B].unsqueeze(2).broadcast_to([B, B, PICK]), ALU.mult))
                assert route_steps[0] == ROUTE_STEPS, route_steps

            def batch(b, with_tail):
                for i in range(CH):
                    n = hidden_of(b, i)
                    if i == MLP_CHUNKS:
                        dve.wait_ge(mine_staged, b + 1)
                    m = i // MLP_CHUNKS
                    hidden(b, n, weight=mine[:, m - 1:m] if m else None)
                    if i + SPLIT_AHEAD < CH:
                        split(b, i + SPLIT_AHEAD)
                    hidden_lo(b, n)
                    if first(b) and i == 0:
                        route_shares()
                    if first(b) and i in PREP_AT:
                        prep(PREP_AT[i])
                    if first(b) and i == L3_OPERAND_AT:
                        l3_operand()
                    if first(b) and i == L3_LO_AT:
                        l3_operand_lo()
                    if with_tail:
                        if i == 0:
                            x1(b)
                            weights_split_lo(b - 1, 3, ca_hi, ca_lo, tail[:, 1, :])
                            stage_mine(b)
                            stage_bias1(b)
                        if i == L1_AFTER:
                            l1_chunks(b, n + 1)
                        if i == X2_AT:
                            x2(b, hidden_of(b, L1_AFTER) + C1)
                        if i == OUT_AT:
                            output(b)
                    if i == C_AT:
                        c3_sum(b)
                        weights_split_lo(b, 1, c3_hi, c3_lo, c3[:, :])
                    if A_FROM <= i <= A_FROM + E + 1:
                        a2_steps(b, i)
                    if i == A_SPLIT_AT:
                        weights_split_lo(b, 2, a2_hi, a2_lo, a2[:, :])
                    if turned(i) is not None:
                        turn_chunk(b, turned(i))
                    if turned(i - 1) is not None:
                        turn_chunk_lo(b, turned(i - 1))
                    if i == XSUM_AT:
                        x_sum(b)

            nc.vector.memset(warm, 0.0).then_inc(warm_ready, 1)
            nc.vector.memset(ones[:, :], 1.0).then_inc(const_dve, 1)
            route_maximum()
            route_top2()
            def first_x_lo(k):
                dve.wait_ge(x_hi_ready, k + 1)
                return nc.vector.tensor_tensor(x_lo[:, k, 0:S], tail[:, k, :], x_hi[:, k, 0:S].bitcast(F32), ALU.subtract)

            dve.wait_ge(first_hi, 1)
            nc.vector.tensor_tensor(res_lo[:, 0, 0:4], raw[:, raw_slot(0), 0:4, 0:P], res_hi[:, 0, 0:4].bitcast(F32),
                                    ALU.subtract).then_inc(first_lo, 1)
            first_x_lo(0)
            first_x_lo(1).then_inc(tail_free, 1)
            dve.wait_ge(split_hi, 1)
            nc.vector.tensor_tensor(res_lo[:, 0, 4:6], raw[:, raw_slot(0), 4:6, 0:P], res_hi[:, 0, 4:6].bitcast(F32),
                                    ALU.subtract).then_inc(split_lo, 1)
            split(0, 1)
            batch(0, False)
            with dve.Fori(1, B) as b:
                batch(b, True)
            stage_bias1(B)
            dve.wait_ge(xsum_ready, 2 * B)
            end_highs(0, out0, ((bank0_done, 1), (down_done, hiddens_before(B))))
            end_floats(0, 0, out0)
            end_lows(0, 0)
            weights_split_lo(B - 1, 3, ca_hi, ca_lo, tail[:, 1, :])
            dve.wait_ge(bias1_staged, B)
            last_tail()

        @block.tensor
        def _(pe):
            def product(out, w_hi_, w_lo_, v_hi, v_lo, start, stop):
                nc.tensor.matmul(out, w_hi_, v_hi, start=start, stop=False)
                nc.tensor.matmul(out, w_hi_, v_lo, start=False, stop=False)
                return nc.tensor.matmul(out, w_lo_, v_hi, start=False, stop=stop)

            def gate_up(b, n, weights, v_hi, v_lo):
                hi, lo = weights
                wait_pair_free(b, n)
                for bank, row, done in ((bank_a, 0, a_ready), (bank_b, 2, b_ready)):
                    for k in range(KD):
                        ins = product(bank[n % 2][:, :], hi[:, row + k], lo[:, row + k], v_hi(k), v_lo(k),
                                      k == 0, k == KD - 1)
                    ins.then_inc(done, 1)

            def down(b, n, weights, banks, start, stop):
                hi, lo = weights
                pe.wait_ge(hid_hi_ready, hiddens_before(b) + n + 1)
                for j in range(KD):
                    nc.tensor.matmul(banks[:, j, :], hi[:, 4 + j], hid_hi[:, n % 2], start=start, stop=False)
                    nc.tensor.matmul(banks[:, j, :], lo[:, 4 + j], hid_hi[:, n % 2], start=False, stop=False)
                pe.wait_ge(hid_lo_ready, hiddens_before(b) + n + 1)
                for j in range(KD):
                    ins = nc.tensor.matmul(banks[:, j, :], hi[:, 4 + j], hid_lo[:, n % 2], start=False, stop=stop)
                ins.then_inc(down_done, 1)

            def wait_pair_free(b, n):
                if n >= 2 or not first(b):
                    pe.wait_ge(hid_ready, hiddens_before(b) + n - 1)

            def first_gate_up():
                (hi, lo), cols = split_slots(0), slice(0, S)
                banks = ((bank_a[0][:, :], 0), (bank_b[0][:, :], 2))
                pe.wait_ge(first_hi, 1)
                for k in range(KD):
                    pe.wait_ge(x_hi_ready, k + 1)
                    for bank, n in banks:
                        nc.tensor.matmul(bank, hi[:, n + k], x_hi[:, k, cols], start=k == 0, stop=False)
                pe.wait_ge(first_lo, 1)
                for bank, n in banks:
                    for k in range(KD):
                        nc.tensor.matmul(bank, lo[:, n + k], x_hi[:, k, cols], start=False, stop=False)
                pe.wait_ge(tail_free, 1)
                for (bank, n), done in zip(banks, (a_ready, b_ready)):
                    for k in range(KD):
                        ins = nc.tensor.matmul(bank, hi[:, n + k], x_lo[:, k, cols], start=False, stop=k == KD - 1)
                    ins.then_inc(done, 1)

            def l0_gate_up(b, i):
                if first(b) and i == 0:
                    return first_gate_up()
                if i >= 2 or first(b):
                    pe.wait_ge(split_lo, splits_done(b, i))
                gate_up(b, hidden_of(b, i), split_slots(i),
                        lambda k: x_hi[:, k, batch_cols(b)], lambda k: x_lo[:, k, batch_cols(b)])

            def l0_down(b, i):
                if i == 0 and not first(b):
                    pe.wait_ge(xs_ready, 4 * (b - 1) + 2)
                down(b, hidden_of(b, i), split_slots(i), out0, i == 0, i == CH - 1)

            def last_down(b):
                down(b, -1, split_slots(CH - 1), out0, False, True)

            def last_down_banks():
                hi, lo = split_slots(CH - 1)
                tile = (hiddens_before(B) - 1) % 2
                pe.wait_ge(hid_lo_ready, hiddens_before(B))
                for j, done in ((0, bank0_done), (1, down_done)):
                    product(out0[:, j, :], hi[:, 4 + j], lo[:, 4 + j], hid_hi[:, tile], hid_lo[:, tile], False, True)\
                        .then_inc(done, 1)

            def l1_gate_up(b, c, n):
                if c == 0:
                    pe.wait_ge(turn_lo, C1 * b)
                    pe.wait_ge(xs_lo_ready, 4 * (b - 1) + 2)
                gate_up(b, n, (w1_hi[:, c], w1_lo[:, c]), lambda k: xs_hi[:, k], lambda k: xs_lo[:, k])

            def l1_down(b, c, n):
                if c == 0:
                    pe.wait_ge(weights_lo, 3 * b)
                down(b, n, (w1_hi[:, c], w1_lo[:, c]), tail, c == 0, c == C1 - 1)

            def c_product(b):
                if first(b):
                    pe.wait_ge(tail_free, len(PREPS))
                    pe.wait_ge(l3_lo, 1)
                else:
                    pe.wait_ge(out_ready, 2 * b)
                for k in range(KD):
                    rows, cols = slice(k * P, (k + 1) * P), bass.ds(b * D, D)
                    ins = product(tail[:, 0, k * D:(k + 1) * D], a3_hi[:, rows], a3_lo[:, rows],
                                  b3_y_hi[:, cols], b3_y_lo[:, cols], True, True)
                ins.then_inc(tail_ready, 1)

            def ca_product(b):
                pe.wait_ge(weights_lo, 3 * b + 2)
                for j in range(KD):
                    for k in range(KD):
                        rows = slice(k * D + j * P, k * D + (j + 1) * P)
                        cols = slice(k * D, (k + 1) * D)
                        ins = product(tail[:, 1, j * D:(j + 1) * D], a2_hi[:, rows], a2_lo[:, rows],
                                      c3_hi[:, cols], c3_lo[:, cols], k == 0, k == KD - 1)
                ins.then_inc(tail_ready, 1)

            def x4_tiles(tiles, bank_of):
                for q in tiles:
                    rows = slice(q * P, (q + 1) * P)
                    for k in range(KD):
                        cols = slice(k * D, (k + 1) * D)
                        ins = product(bank_of(q), xs_hi[:, k, rows], xs_lo[:, k, rows], ca_hi[:, cols], ca_lo[:, cols],
                                      k == 0, k == KD - 1)
                return ins

            def x4(b):
                pe.wait_ge(xs_lo_ready, 4 * (b - 1) + 4)
                x4_tiles(range(NQ), lambda q: tail[:, q // 2, (q % 2) * D:(q % 2 + 1) * D]).then_inc(tail_ready, 1)

            def last_tail():
                def first_halves():
                    items = ((0, 0), (0, 2), (1, 0), (1, 2))
                    place = lambda m, n: (bank_b if n else bank_a)[m][:, 0:HALF]
                    for k in range(KD):
                        pe.wait_ge(end_hi, k + 1)
                        for m, n in items:
                            if k == 0 and n == 0:
                                pe.wait_ge(hid_ready, hiddens_before(B) + m - 1)
                            nc.tensor.matmul(place(m, n), w1_hi[:, m, n + k], xs_hi[:, k, 0:HALF], start=k == 0, stop=False)
                            nc.tensor.matmul(place(m, n), w1_lo[:, m, n + k], xs_hi[:, k, 0:HALF], start=False, stop=False)
                    pe.wait_ge(end_lo, KD)
                    for m, n in items:
                        for k in range(KD):
                            ins = nc.tensor.matmul(place(m, n), w1_hi[:, m, n + k], xs_lo[:, k, 0:HALF],
                                                   start=False, stop=k == KD - 1)
                        ins.then_inc(b_ready if n else a_ready, 1)

                def gate_up_half(m):
                    h, c = m // C1, m % C1
                    cols = slice(h * HALF, (h + 1) * HALF)
                    pe.wait_ge(end_lo, KD * (h + 1))
                    for bank, n, done, left in ((bank_a, 0, a_ready, act_ready), (bank_b, 2, b_ready, hid_ready)):
                        pe.wait_ge(left, hiddens_before(B) + m - 1)
                        for k in range(KD):
                            ins = product(bank[m % 2][:, 0:HALF], w1_hi[:, c, n + k], w1_lo[:, c, n + k],
                                          xs_hi[:, k, cols], xs_lo[:, k, cols], k == 0, k == KD - 1)
                        ins.then_inc(done, 1)

                def down_half(m):
                    h, c = m // C1, m % C1
                    cols, slot = slice(h * HALF, (h + 1) * HALF), half_slot(m)
                    pe.wait_ge(hid_lo_ready, hiddens_before(B) + m + 1)
                    for j in range(KD):
                        ins = product((tail, out0)[h][:, j, cols], w1_hi[:, c, 4 + j], w1_lo[:, c, 4 + j],
                                      hid_hi[slot], hid_lo[slot], c == 0, c == C1 - 1)
                        if m == 2 * C1 - 1 and j == 0:
                            ins.then_inc(bank0_done, 1)
                    ins.then_inc(down_done, 1)

                def last_x4():
                    tiles = ((bank_a[1][:, 0:D], 2), (bank_b[1][:, 0:D], 3))
                    rows = lambda q: slice(q * P, (q + 1) * P)
                    for k in range(KD):
                        cols = slice(k * D, (k + 1) * D)
                        pe.wait_ge(end_half1, KD + k + 1)
                        for bank, q in tiles:
                            nc.tensor.matmul(bank, xs_hi[:, k, rows(q)], ca_hi[:, cols], start=k == 0, stop=False)
                            nc.tensor.matmul(bank, xs_hi[:, k, rows(q)], ca_lo[:, cols], start=False, stop=False)
                    pe.wait_ge(end_lo, 4 * KD)
                    for bank, q in tiles:
                        for k in range(KD):
                            ins = nc.tensor.matmul(bank, xs_lo[:, k, rows(q)], ca_hi[:, k * D:(k + 1) * D],
                                                   start=False, stop=k == KD - 1)
                        ins.then_inc(end_rows, 1)

                pe.wait_ge(turn_lo, C1 * B)
                first_halves()
                for m in range(2, 2 * C1):
                    gate_up_half(m)
                    if m == 2:
                        pe.wait_ge(weights_lo, 3 * B)
                    down_half(m - 2)
                down_half(2 * C1 - 2)
                pe.wait_ge(end_lo, 3 * KD)
                pe.wait_ge(hid_ready, hiddens_before(B) + 2 * C1 - 1)
                place = lambda q: bank_a[0][:, q * D:(q + 1) * D]
                x4_tiles((0,), place)
                down_half(2 * C1 - 1)
                x4_tiles((1,), place).then_inc(end_rows, 1)
                last_x4()

            def prep(what):
                use = PREPS.index(what)
                wait(pe, tail_free, use)
                one = lambda out, lhs, rhs: nc.tensor.matmul(out, lhs, rhs, start=True, stop=True)
                if what[0] == "x":
                    b = what[1]
                    if b:
                        pe.wait_ge(x_in[b], 16)
                    for k in range(KD):
                        if b == 0:
                            pe.wait_ge(x0_in[k], 16)
                        for q in range(NQ):
                            ins = nc.tensor.transpose(tail[:, k, q * P:(q + 1) * P], x_nat[:, b, q, k * P:(k + 1) * P],
                                                      ident[:, :])
                        if b == 0 and k == 0:
                            ins.then_inc(x0_turned, 1)
                elif what[0] == "route":
                    pe.wait_ge(route_step, ROUTE_STEPS)
                    one(tail[:, 0, 0:B * PICK], ones[:, :], pick_diag[:, :, :].rearrange("p b n -> p (b n)"))
                    ins = one(tail[0:E, 1, 0:B], logits[:, :], ident[0:B, 0:B])
                elif what[0] == "turn":
                    one(tail[:, 0, D:D + B], expand[:, :], cond_t[:, :])
                    pe.wait_ge(turn_in, 48)
                    for j in range(KD):
                        nc.tensor.transpose(tail[:, 0, j * P:(j + 1) * P], b3_nat[:, j].rearrange("o e r -> o (e r)"),
                                            ident[:, :])
                    for k in range(KD):
                        for j in range(KD):
                            ins = nc.tensor.transpose(tail[:, 1, (k * KD + j) * P:(k * KD + j + 1) * P],
                                                      base_nat[:, j, k * P:(k + 1) * P], ident[:, :])
                elif what[0] == "rows":
                    for n in range(2):
                        ins = one(tail[:, n, :], ones[:, :], bias_diag[:, 2 * n:2 * n + 2].rearrange("p b d -> p (b d)"))
                else:
                    rows = tail[0:B, 0, 0:D]
                    nc.tensor.matmul(rows, u3_y[:, :], b3_t[:, :], start=True, stop=False)
                    for k in range(KD):
                        ins = nc.tensor.matmul(rows, bias2_m[:, k], base_t[:, k], start=False, stop=k == KD - 1)
                ins.then_inc(tail_ready, 1)

            def batch(b, with_tail):
                for i in range(CH):
                    l0_gate_up(b, i)
                    if first(b) and i in PREP_AT:
                        prep(PREP_AT[i])
                    if i == 0:
                        if with_tail:
                            last_down(b)
                    elif with_tail and i == X2_AT:
                        l1_down(b, C1 - 1, hidden_of(b, L1_AFTER) + C1)
                    else:
                        l0_down(b, i - 1)
                    if with_tail:
                        if i == L1_AFTER:
                            n0 = hidden_of(b, i)
                            for c in range(C1):
                                l1_gate_up(b, c, n0 + 1 + c)
                                if c == 0:
                                    l0_down(b, i)
                                else:
                                    l1_down(b, c - 1, n0 + c)
                        if i == OUT_AT:
                            x4(b)
                    if i == C_AT:
                        c_product(b)
                    if i == CA_AT:
                        ca_product(b)

            def warm_up(times):
                for _ in range(times):
                    nc.tensor.matmul(out0[:, 0, 0:P], warm, warm, start=True, stop=True)

            pe.wait_ge(warm_ready, 1)
            warm_up(WARM[0])
            pe.wait_ge(const_pool, 5)
            pe.wait_ge(const_dve, 1)
            prep(("x", 0))
            warm_up(WARM[1])
            batch(0, False)
            with pe.Fori(1, B) as b:
                batch(b, True)
            last_down_banks()
            last_tail()


INPUTS = ["x", "cond_8", "L0_cond_skill_gate", "L0_cond_skill_up", "L0_cond_skill_down", "L0_cond_shared_gate",
          "L0_cond_shared_up", "L0_cond_shared_down", "L1_cond_W_up", "L1_cond_b_up", "L1_cond_W_gate",
          "L1_cond_b_gate", "L1_cond_W_down", "L1_cond_b_down", "L2_cond_weight", "L2_cond_mask", "L2_cond_bias",
          "L3_cond_W_base", "L3_cond_b_base", "L3_cond_As", "L3_cond_Bs"]


def kernel(**inputs):
    import numpy as np
    import concourse.bacc as bacc
    from concourse import mybir
    from concourse.bass_utils import run_bass_kernel_spmd

    nc = bacc.Bacc("TRN2", target_bir_lowering=False, num_devices=1)
    arrays, tensors = {}, {}
    for name in INPUTS:
        a = np.ascontiguousarray(inputs[name])
        arrays[f"in_{name}"] = a
        tensors[name] = nc.dram_tensor(f"in_{name}", a.shape, mybir.dt.from_np(a.dtype), kind="ExternalInput").ap()
    tensors["out"] = nc.dram_tensor("out_x4", (B, S, D), mybir.dt.float32, kind="ExternalOutput").ap()
    build(nc, tensors)
    result = run_bass_kernel_spmd(nc, [arrays], core_ids=[0])
    return result.results[0]["out_x4"]
```
